# Optimizing a Trainium2 kernel written in Bass

```python
import numpy as np
import jax
import jax.numpy as jnp

def _softmax(x, axis=-1):
    return jax.nn.softmax(x, axis=axis)

def _gelu(x):
    return jax.nn.gelu(x, approximate=True)

def _silu(x):
    return jax.nn.silu(x)

def _sigmoid(x):
    return jax.nn.sigmoid(x)

def _layernorm(x, axis=-1, eps=1e-05):
    m = jnp.mean(x, axis=axis, keepdims=True)
    v = jnp.var(x, axis=axis, keepdims=True)
    return (x - m) / jnp.sqrt(v + eps)

def _scatter_add(tgt, idx, src, axis=0):
    return tgt.at[idx].add(src)

def _segment_sum(src, seg, n):
    return jax.ops.segment_sum(src, seg, n)
kernel_name = 'mk_sandwich_d1_jaxref_r8_905c07'

def setup_inputs(seed: int=0):
    np.random.seed(seed)
    _w = jnp.asarray

    def _L0_attn_setup():
        import jax, jax.numpy as jnp
        import numpy as np
        import math
        EMBED_DIM = 256
        N_HEADS = 16
        HEAD_DIM = EMBED_DIM // N_HEADS
        THETA_BASE = 10000.0

        def _rope_freqs(seq_len):
            i = jnp.arange(HEAD_DIM // 2, dtype=jnp.float32)
            inv_freq = 1.0 / THETA_BASE ** (2.0 * i / HEAD_DIM)
            pos = jnp.arange(seq_len, dtype=jnp.float32)
            th = jnp.outer(pos, inv_freq)
            return (jnp.cos(th), jnp.sin(th))

        def _rope(t, cos, sin):
            b, h, s, d = t.shape
            tr = t.reshape(b, h, s, d // 2, 2)
            x0, x1 = (tr[..., 0], tr[..., 1])
            r0 = x0 * cos - x1 * sin
            r1 = x0 * sin + x1 * cos
            return jnp.stack([r0, r1], axis=-1).reshape(b, h, s, d)
        key = jax.random.key(seed)
        k1, k2, k3 = jax.random.split(key, 3)
        B, S = (2, 256)
        x = jax.random.normal(k1, (B, S, EMBED_DIM), jnp.float32)
        scale = EMBED_DIM ** (-0.5)
        Wqkv = jax.random.normal(k2, (EMBED_DIM, 3 * EMBED_DIM), jnp.float32) * scale
        Wo = jax.random.normal(k3, (EMBED_DIM, EMBED_DIM), jnp.float32) * scale
        return {'x': x, 'Wqkv': Wqkv, 'Wo': Wo}
    _L0_attn_in = _L0_attn_setup()

    def _L0_ffn_setup():
        import jax, jax.numpy as jnp
        import numpy as np
        E = 32
        K = 8
        H = 256
        F = 96
        B, S = (1, 128)

        def _moe(x, wg, w1, v1, w2):
            T = x.shape[0]
            logits = x @ wg.T
            scores = jax.nn.softmax(logits, axis=-1)
            weights, idx = jax.lax.top_k(scores, K)
            weights = weights / jnp.sum(weights, axis=-1, keepdims=True)
            flat_e = idx.reshape(-1)
            flat_t = jnp.repeat(jnp.arange(T), K)
            flat_w = weights.reshape(-1)
            order = jnp.argsort(flat_e)
            e_s = flat_e[order]
            t_s = flat_t[order]
            w_s = flat_w[order]
            group_sizes = jnp.bincount(e_s, length=E).astype(jnp.int32)
            xs = x[t_s]
            g = jax.lax.ragged_dot(xs, w1, group_sizes)
            u = jax.lax.ragged_dot(xs, v1, group_sizes)
            h = jax.nn.silu(g) * u
            ys = jax.lax.ragged_dot(h, w2, group_sizes)
            out = jnp.zeros((T, x.shape[1]), x.dtype).at[t_s].add(ys * w_s[:, None])
            return out
        key = jax.random.key(seed)
        k0, k1, k2, k3, k4 = jax.random.split(key, 5)
        scale = 0.02
        return {'hidden_states': jax.random.normal(k0, (B, S, H), jnp.float32), 'wg': jax.random.normal(k1, (E, H), jnp.float32) * scale, 'w1': jax.random.normal(k2, (E, H, F), jnp.float32) * scale, 'v1': jax.random.normal(k3, (E, H, F), jnp.float32) * scale, 'w2': jax.random.normal(k4, (E, F, H), jnp.float32) * scale}
    _L0_ffn_in = _L0_ffn_setup()
    _d = {'L0_attn_x': _L0_attn_in['x'], 'L0_attn_Wqkv': _L0_attn_in['Wqkv'], 'L0_attn_Wo': _L0_attn_in['Wo'], 'L0_ffn_wg': _L0_ffn_in['wg'], 'L0_ffn_w1': _L0_ffn_in['w1'], 'L0_ffn_v1': _L0_ffn_in['v1'], 'L0_ffn_w2': _L0_ffn_in['w2']}
    _x0 = _d['L0_attn_x']
    _d['L0_attn_x'] = jax.random.normal(jax.random.fold_in(jax.random.key(seed), 1), (4, 512, 256), dtype=_x0.dtype)
    del _x0
    return _d

def reference(L0_attn_x, L0_attn_Wqkv, L0_attn_Wo, L0_ffn_wg, L0_ffn_w1, L0_ffn_v1, L0_ffn_w2):

    def _L0_attn_ref(x, Wqkv, Wo):
        import jax, jax.numpy as jnp
        import numpy as np
        import math
        EMBED_DIM = 256
        N_HEADS = 16
        HEAD_DIM = EMBED_DIM // N_HEADS
        THETA_BASE = 10000.0

        def _rope_freqs(seq_len):
            i = jnp.arange(HEAD_DIM // 2, dtype=jnp.float32)
            inv_freq = 1.0 / THETA_BASE ** (2.0 * i / HEAD_DIM)
            pos = jnp.arange(seq_len, dtype=jnp.float32)
            th = jnp.outer(pos, inv_freq)
            return (jnp.cos(th), jnp.sin(th))

        def _rope(t, cos, sin):
            b, h, s, d = t.shape
            tr = t.reshape(b, h, s, d // 2, 2)
            x0, x1 = (tr[..., 0], tr[..., 1])
            r0 = x0 * cos - x1 * sin
            r1 = x0 * sin + x1 * cos
            return jnp.stack([r0, r1], axis=-1).reshape(b, h, s, d)
        B, S, E = x.shape
        H, D = (N_HEADS, E // N_HEADS)
        qkv = x @ Wqkv
        q, k, v = jnp.split(qkv, 3, axis=-1)
        heads = lambda t: t.reshape(B, S, H, D).transpose(0, 2, 1, 3)
        q, k, v = (heads(q), heads(k), heads(v))
        cos, sin = _rope_freqs(S)
        q = _rope(q, cos, sin)
        k = _rope(k, cos, sin)
        scores = jnp.einsum('bhqd,bhkd->bhqk', q, k) / math.sqrt(D)
        causal = jnp.tril(jnp.ones((S, S), dtype=bool))
        scores = jnp.where(causal, scores, -jnp.inf)
        attn = jax.nn.softmax(scores, axis=-1)
        op = jnp.einsum('bhqk,bhkd->bhqd', attn, v)
        op = op.transpose(0, 2, 1, 3).reshape(B, S, E)
        return op @ Wo

    def _L0_ffn_ref(hidden_states, wg, w1, v1, w2):
        import jax, jax.numpy as jnp
        import numpy as np
        E = 32
        K = 8
        H = 256
        F = 96
        B, S = (1, 128)

        def _moe(x, wg, w1, v1, w2):
            T = x.shape[0]
            logits = x @ wg.T
            scores = jax.nn.softmax(logits, axis=-1)
            weights, idx = jax.lax.top_k(scores, K)
            weights = weights / jnp.sum(weights, axis=-1, keepdims=True)
            flat_e = idx.reshape(-1)
            flat_t = jnp.repeat(jnp.arange(T), K)
            flat_w = weights.reshape(-1)
            order = jnp.argsort(flat_e)
            e_s = flat_e[order]
            t_s = flat_t[order]
            w_s = flat_w[order]
            group_sizes = jnp.bincount(e_s, length=E).astype(jnp.int32)
            xs = x[t_s]
            g = jax.lax.ragged_dot(xs, w1, group_sizes)
            u = jax.lax.ragged_dot(xs, v1, group_sizes)
            h = jax.nn.silu(g) * u
            ys = jax.lax.ragged_dot(h, w2, group_sizes)
            out = jnp.zeros((T, x.shape[1]), x.dtype).at[t_s].add(ys * w_s[:, None])
            return out
        Bb, Ss, Hh = hidden_states.shape
        x = hidden_states.reshape(Bb * Ss, Hh)
        out = _moe(x, wg, w1, v1, w2)
        return out.reshape(Bb, Ss, Hh)
    x = L0_attn_x
    x = x + _layernorm(_L0_attn_ref(_layernorm(x, axis=-1), L0_attn_Wqkv, L0_attn_Wo), axis=-1)
    x = x + _layernorm(_L0_ffn_ref(_layernorm(x, axis=-1), L0_ffn_wg, L0_ffn_w1, L0_ffn_v1, L0_ffn_w2), axis=-1)
    return x

_drawn_inputs = setup_inputs


def setup_inputs(seed=0):
    import zlib

    import numpy as np

    out = dict(_drawn_inputs(seed))
    spreads = {}
    factors = {}
    for name, (base, spread) in spreads.items():
        noise = np.random.default_rng([zlib.crc32(name.encode()), seed]).standard_normal(out[name].shape)
        drawn = base * np.exp(spread * noise) if base else spread * noise
        out[name] = jnp.asarray(drawn.astype(out[name].dtype))
    for name, factor in factors.items():
        out[name] = (out[name] * factor).astype(out[name].dtype)
    return out
```

```python
import concourse.bass as bass
from concourse import mybir
from contextlib import ExitStack

F32 = mybir.dt.float32
F32R = mybir.dt.float32r
BF16 = mybir.dt.bfloat16
ACTF = mybir.ActivationFunctionType
ALU = mybir.AluOpType
AXX = mybir.AxisListType.X

P = 128
BATCHES, SEQ, EMB = 4, 512, 256
TOKENS = BATCHES * SEQ
TILES = TOKENS // P
QT = SEQ // P
KC = EMB // P
HEADS, HD = 16, 16
HALF = HEADS // 2
ROWS = 4 * HD + 2
VW = 2 * HD + 2
EXPERTS, TOPK, FF = 32, 8, 96
CHUNKS = TOKENS // 512
EPS = 1e-5

PAIR_BANKS = [[(0, 3, 0)], [(0, 2, 0), (0, 0, 384)], [(0, 1, 0), (1, 1, 256)], [(1, 3, 0)], [(1, 2, 0), (1, 0, 384)]]
NPAIR = HALF // 2
NC = len(PAIR_BANKS) * NPAIR
KPLACE = {(h, 3 - r): (w, col) for w, bank in enumerate(PAIR_BANKS) for h, r, col in bank}
POOL_LOW = (0, 2, 4)
CLOSE_AT = {1: 0, 2: 0, 3: 1, 4: 1, 5: 2, 6: 3, 7: 4, 8: 5, 9: 5, 10: 6, 11: 7, 12: 7, 13: 8}
PROJECT_AT = {0: 0, 1: 0, 2: 1, 3: 1, 4: 2, 5: 3, 6: 3, 7: 4}


def low_count(u, c, by_pool):
    mine = [w in POOL_LOW for w in range(5)] if by_pool else [w not in POOL_LOW for w in range(5)]
    n = (c // 5) * sum(mine) + sum(mine[:c % 5])
    return u * NPAIR * sum(mine) + n


def close_steps(pos):
    return [(i, s) for i in range(QT) for s, at in CLOSE_AT.items() if 5 + 2 * i + at == pos]


def project_steps(pos):
    return [(i, s) for i in range(QT) for s, at in PROJECT_AT.items() if 1 + 2 * i + at == pos]


def half_slot(f, c):
    return (f * NC + c) % 8


def early_scores(pos):
    return [c for c in range(NC) if 4 + c * 12 // NC == pos]


def late_scores(pos):
    return [c for c in range(NC) if 13 + c * 5 // NC == pos]


def wait(engine, sem, value):
    if not isinstance(value, int) or value > 0:
        engine.wait_ge(sem, value)


def build(nc, x, wqkv, wo, wgT, w13, w2, ident, mask, rope, out):
    ctx = ExitStack()
    with ctx:
        def sb(name, shape, dt=F32):
            return ctx.enter_context(nc.sbuf_tensor(name, shape, dt))

        def sem(name):
            return ctx.enter_context(nc.semaphore(name))

        def f32(ap):
            return ap.bitcast(F32)

        qk_dram = nc.dram_tensor("qk_dram", (2, P, 4, SEQ), F32).ap()
        max_dram = nc.dram_tensor("max_dram", (2, QT, 2, HALF, P), F32).ap()

        xt = sb("xt", [P, TILES, EMB])
        x2T = sb("x2T", [P, KC, TOKENS])
        gates = sb("gates", [P, TILES, EXPERTS])
        half = sb("half", [P, QT])

        ph1 = ExitStack()
        ph1.__enter__()

        def sb1(name, shape, dt=F32):
            return ph1.enter_context(nc.sbuf_tensor(name, shape, dt))

        ident_f = sb1("ident_f", [P, P])
        ident_b = sb1("ident_b", [P, P], BF16)
        mask_b = sb1("mask_b", [P, P], BF16)
        wqkvh = sb1("wqkvh", [P, KC, 3 * EMB], F32R)
        wqkvl = sb1("wqkvl", [P, KC, 3 * EMB], F32R)
        woh = sb1("woh", [P, KC, EMB], F32R)
        wol = sb1("wol", [P, KC, EMB], F32R)
        wgh = sb1("wgh", [P, KC, EXPERTS], F32R)
        wgl = sb1("wgl", [P, KC, EXPERTS], F32R)
        rope_sb = sb1("rope_sb", [P, QT, 2, 2, HD])
        ln1_stat = sb1("ln1_stat", [P, QT, 6])
        ln1_mv = sb1("ln1_mv", [P, QT, 2])
        ln1_var = sb1("ln1_var", [P, QT])
        ln1_rstd = sb1("ln1_rstd", [P, QT])
        xn = sb1("xn", [P, EMB])
        xnTh = sb1("xnTh", [P, KC, P], F32R)
        xnTl = sb1("xnTl", [P, KC, P], F32R)
        rope_cos = sb1("rope_cos", [P, 2, HEADS, HD])
        rope_sin = sb1("rope_sin", [P, 2, HEADS, HD])
        qkTh = sb1("qkTh", [P, 4, P], F32R)
        qkTl = sb1("qkTl", [P, 4, P], F32R)
        v_stage = sb1("v_stage", [P, QT, HEADS, HD])
        vs = sb1("vs", [P, 2, QT, NPAIR, 3, VW], F32R)
        qs = [sb1(f"qs{f}", [ROWS, HALF, SEQ], F32R) for f in range(2)]
        ks = [sb1(f"ks{f}", [ROWS, HALF, SEQ], F32R) for f in range(2)]
        probs = sb1("probs", [P, 4, 512])
        probsh = sb1("probsh", [P, 8, 512], F32R)
        probsl = sb1("probsl", [P, 8, 512], F32R)
        wqkv_f = probs[:, 0:3].rearrange("p a n -> p (a n)").rearrange("p (c n) -> p c n", c=KC)
        wo_f = probs[:, 3].rearrange("p (c n) -> p c n", c=KC)
        wg_f = v_stage[:, 0].rearrange("p h d -> p (h d)")[:, 0:KC * EXPERTS].rearrange("p (c n) -> p c n", c=KC)
        mask_f = v_stage[:, 1].rearrange("p h d -> p (h d)")[:, 0:P]
        negmax = sb1("negmax", [P, QT, HALF])
        maxhl = sb1("maxhl", [P, 2, QT, 2, HALF])
        maxT = sb1("maxT", [P, P])
        oT = sb1("oT", [P, SEQ])
        zeros = oT[P - 2:P]
        o_raw = sb1("o_raw", [P, 2, QT, VW])
        o_inv = sb1("o_inv", [P, 2, QT])
        o_sum = sb1("o_sum", [P, 2, QT, HD])
        attn_first = sb1("attn_first", [P, QT, HALF, HD])
        attn = sb1("attn", [P, QT, HEADS, HD])
        attnTh = sb1("attnTh", [P, 2, KC, P], F32R)
        attnTl = sb1("attnTl", [P, 2, KC, P], F32R)
        y_sb = sb1("y_sb", [P, 2, EMB])
        xn2 = y_sb
        post_stat = sb1("post_stat", [P, 2, 6])
        post_mv = sb1("post_mv", [P, 2, 2])
        post_var = sb1("post_var", [P, 2])
        post_rstd = sb1("post_rstd", [P, 2])
        xh_tile = sb1("xh_tile", [P, 2, KC, P], F32R)
        xl_tile = sb1("xl_tile", [P, 2, KC, P], F32R)
        logits = sb1("logits", [P, 2, EXPERTS])
        top = sb1("top", [P, 2, TOPK])
        negtop = sb1("negtop", [P, 2])
        struck = sb1("struck", [P, 2, EXPERTS])
        chosen = sb1("chosen", [P, 2, EXPERTS])
        expl = sb1("expl", [P, 2, EXPERTS])
        picked = sb1("picked", [P, 2, EXPERTS])
        gsum = sb1("gsum", [P, 2])
        ginv = sb1("ginv", [P, 2])
        ph1.close()

        xh = sb("xh", [P, KC, TOKENS], F32R)
        xl = sb("xl", [P, KC, TOKENS], F32R)
        acc = sb("acc", [P, TILES, EMB])
        w13f = sb("w13f", [P, 2, KC, 2 * FF])
        w2f = sb("w2f", [FF, 2, EMB])
        w13h = sb("w13h", [P, 2, KC, 2 * FF], F32R)
        w13l = sb("w13l", [P, 2, KC, 2 * FF], F32R)
        w2h = sb("w2h", [FF, 2, EMB], F32R)
        w2l = sb("w2l", [FF, 2, EMB], F32R)
        silu = sb("silu", [FF, 2, 512])
        hid = sb("hid", [FF, 2, 512])
        hidh = sb("hidh", [FF, 4, 512], F32R)
        hidl = sb("hidl", [FF, 4, 512], F32R)
        fin_stat = sb("fin_stat", [P, TILES, 6])
        fin_mv = sb("fin_mv", [P, TILES, 2])
        fin_var = sb("fin_var", [P, TILES])
        fin_rstd = sb("fin_rstd", [P, TILES])
        ybuf = sb("ybuf", [P, TILES, EMB])

        bank = [ctx.enter_context(nc.psum_tensor(f"bank{n}", [P, 512], F32)) for n in range(8)]
        SCORE, WEIGH, OB, QK, XT, VB = (0, 1), (2, 3), 4, 5, 6, 7

        s_const = sem("s_const")
        s_x = sem("s_x")
        s_prep = sem("s_prep")
        s_ones = sem("s_ones")
        ln1_bn = sem("ln1_bn"); ln1_mean = sem("ln1_mean"); ln1_eps = sem("ln1_eps")
        ln1_scale = sem("ln1_scale")
        xn_ready = sem("xn_ready")
        xnT_psum = sem("xnT_psum")
        xnTh_ready = sem("xnTh_ready")
        xnTl_ready = sem("xnTl_ready")
        qkv_psum = sem("qkv_psum")
        v_staged = sem("v_staged")
        rope_parts = sem("rope_parts")
        rope_done = sem("rope_done")
        qkT_psum = sem("qkT_psum")
        qkTh_ready = sem("qkTh_ready")
        qkTl_ready = sem("qkTl_ready")
        s_spill = sem("s_spill")
        s_load = sem("s_load")
        vh_ready = sem("vh_ready")
        vl_ready = sem("vl_ready")
        score_psum = sem("score_psum")
        max_done = sem("max_done")
        maxh_ready = sem("maxh_ready"); maxl_ready = sem("maxl_ready")
        maxT_psum = sem("maxT_psum")
        maxT_ready = sem("maxT_ready")
        s_max_out = sem("s_max_out")
        s_max_in = sem("s_max_in")
        weigh_psum = sem("weigh_psum")
        exp_done = sem("exp_done")
        high_done = sem("high_done")
        low_pool = sem("low_pool")
        low_dve = sem("low_dve")
        pv_psum = sem("pv_psum")
        oT_ready = sem("oT_ready")
        o_psum = sem("o_psum")
        o_copied = sem("o_copied")
        inv_ready = sem("inv_ready")
        osum_ready = sem("osum_ready")
        attn_ready = sem("attn_ready")
        joined = sem("joined")
        attnT_psum = sem("attnT_psum")
        attnTh_ready = sem("attnTh_ready")
        attnTl_ready = sem("attnTl_ready")
        wo_psum = sem("wo_psum")
        post_bn = sem("post_bn"); post_mean = sem("post_mean"); post_eps = sem("post_eps")
        post2_bn = sem("post2_bn"); post2_mean = sem("post2_mean"); post2_eps = sem("post2_eps")
        post_scale = sem("post_scale"); post2_scale = sem("post2_scale")
        y_norm = sem("y_norm")
        x1_ready = sem("x1_ready")
        xn2_ready = sem("xn2_ready")
        xn2T_psum = sem("xn2T_psum")
        xh_ready = sem("xh_ready")
        xl_ready = sem("xl_ready")
        x2T_ready = sem("x2T_ready")
        router_psum = sem("router_psum")
        logits_ready = sem("logits_ready")
        top_ready = sem("top_ready"); negtop_ready = sem("negtop_ready")
        struck_ready = sem("struck_ready"); chosen_ready = sem("chosen_ready")
        expl_ready = sem("expl_ready")
        picked_ready = sem("picked_ready"); gsum_ready = sem("gsum_ready")
        ginv_ready = sem("ginv_ready"); gates_ready = sem("gates_ready")
        xh_cut = sem("xh_cut")
        xl_cut = sem("xl_cut")
        w_load = [sem("w_load0"), sem("w_load1")]
        w_split = sem("w_split")
        wh_made = sem("wh_made")
        gu_psum = sem("gu_psum")
        silu_ready = sem("silu_ready")
        hid_ready = sem("hid_ready")
        hidh_ready = sem("hidh_ready")
        hidl_ready = sem("hidl_ready")
        down_psum = sem("down_psum")
        acc_done = sem("acc_done")
        fin_bn = sem("fin_bn"); fin_mean = sem("fin_mean"); fin_eps = sem("fin_eps")
        fin_scale = sem("fin_scale"); fin_norm = sem("fin_norm"); fin_ready = sem("fin_ready")
        s_out = sem("s_out")
        s_spare = sem("s_spare")

        block = ctx.enter_context(nc.Block())
        UNITS = 2 * CHUNKS
        EPAIRS = EXPERTS // 2

        def alone(engine):
            engine.sem_inc(s_spare, 1)

        @block.sync
        def _(sp):
            sp.dma_start(xt[:, 0:QT, :], x[0].rearrange("(t p) e -> p t e", p=P)).then_inc(s_x, 16)
            sp.dma_start(wqkv_f, wqkv.rearrange("(c p) n -> p c n", p=P)).then_inc(s_const, 16)
            sp.dma_start(ident_f[:], ident).then_inc(s_const, 16)
            sp.dma_start(rope_sb[:], rope.rearrange("(t p) a b d -> p t a b d", p=P)).then_inc(s_const, 16)
            sp.dma_start(mask_f, mask).then_inc(s_const, 16)
            sp.dma_start(wo_f, wo.rearrange("(c p) n -> p c n", p=P)).then_inc(s_const, 16)
            sp.dma_start(wg_f, wgT.rearrange("(c p) n -> p c n", p=P)).then_inc(s_const, 16)
            for b in range(1, BATCHES):
                sp.wait_ge(s_x, 16 * b)
                sp.dma_start(xt[:, b * QT:(b + 1) * QT, :],
                             x[b].rearrange("(t p) e -> p t e", p=P)).then_inc(s_x, 16)
            sp.wait_ge(s_ones, 7)

            def spill(b):
                for i in range(QT):
                    t = QT * b + i
                    for c, part, ready in ((0, qkTh, qkTh_ready), (1, qkTl, qkTl_ready)):
                        sp.wait_ge(ready, t + 1)
                        alone(sp)
                        sp.dma_start(qk_dram[c, :, :, i * P:(i + 1) * P], f32(part[:])).then_inc(s_spill, 16)
                    sp.wait_ge(s_spill, 32 * t + 32)
                    alone(sp)

            def load_stacks(b, f):
                u = 2 * b + f
                wait(sp, weigh_psum, (u - 2) * NC + NC)
                alone(sp)
                for stack, w, cuts in ((qs[f], f, (0, 1, 0, 1)), (ks[f], 2 + f, (0, 0, 1, 1))):
                    for r, c in enumerate(cuts):
                        sp.dma_start(f32(stack[r * HD:(r + 1) * HD]),
                                     qk_dram[c, :, w, :].rearrange("(a d) t -> d a t", d=HD)).then_inc(s_load, 16)
                sp.dma_start(f32(qs[f][4 * HD:ROWS]), zeros.unsqueeze(1).broadcast_to([2, HALF, SEQ])
                             ).then_inc(s_load, 16)
                sp.wait_ge(s_load, 144 * u + 144)
                alone(sp)

            def load_maxima(b, f):
                u = 2 * b + f
                sp.wait_ge(maxT_ready, u + 1)
                alone(sp)
                sp.dma_start(max_dram[f].rearrange("i c a t -> (i c a) t"), maxT[f * P // 2:(f + 1) * P // 2]).then_inc(s_max_out, 16)
                sp.wait_ge(s_max_out, 16 * u + 16)
                alone(sp)
                for i in range(QT):
                    sp.dma_start(f32(qs[f][4 * HD:ROWS, :, i * P:(i + 1) * P]), max_dram[f, i]).then_inc(s_max_in, 16)
                sp.wait_ge(s_max_in, 64 * u + 64)
                alone(sp)

            spill(0)
            load_stacks(0, 0)
            load_maxima(0, 0)
            load_stacks(0, 1)
            load_maxima(0, 1)
            with sp.Fori(0, BATCHES - 1) as b:
                spill(b + 1)
                for f in range(2):
                    load_stacks(b + 1, f)
                    load_maxima(b + 1, f)

            sp.wait_ge(gates_ready, TILES)

            def load_expert(e, slot):
                sp.dma_start(w13f[:, slot], w13[bass.ds(e, 1)].rearrange("o (c p) n -> p (o c) n", p=P)
                             ).then_inc(w_load[slot], 16)
                sp.dma_start(w2f[:, slot], w2[bass.ds(e, 1)].rearrange("o f n -> f (o n)")
                             ).then_inc(w_load[slot], 16)

            load_expert(0, 0)
            load_expert(1, 1)
            with sp.Fori(0, EPAIRS - 1) as ep:
                for slot in range(2):
                    sp.wait_ge(w_split, 2 * ep + slot + 1)
                    load_expert(2 * ep + 2 + slot, slot)

            for t in range(TILES):
                sp.wait_ge(fin_ready, t + 1)
                sp.dma_start(out[t // QT, (t % QT) * P:(t % QT + 1) * P, :], ybuf[:, t, :]).then_inc(s_out, 16)
            sp.wait_ge(s_out, 16 * TILES)


        @block.gpsimd
        def _(pool):
            for k, (buffer, value) in enumerate((
                    (maxhl[:], 0.0), (oT[:], 0.0), (f32(ks[0][4 * HD:ROWS]), 1.0), (f32(ks[1][4 * HD:ROWS]), 1.0),
                    (f32(vs[:]), 0.0), (f32(vs[:, 0, :, :, 0::2, 2 * HD]), 1.0), (f32(vs[:, 1, :, :, 0::2, 2 * HD]), 1.0))):
                if k:
                    pool.wait_ge(s_ones, k)
                nc.gpsimd.memset(buffer, value).then_inc(s_ones, 1)
            pool.sem_inc(low_pool, 4)
            pool.wait_ge(s_prep, 1)

            def project(b, i, step):
                t = b * QT + i
                if step == 5:
                    pool.wait_ge(rope_parts, t + 1)
                    nc.gpsimd.tensor_tensor(rope_cos[:], rope_cos[:], rope_sin[:], ALU.add).then_inc(rope_done, 1)

            def close(b, i, step):
                T, r = b * QT + i, i % 2
                if step == 5:
                    pool.wait_ge(post_eps, T + 1)
                    nc.gpsimd.tensor_tensor(post_rstd[:, r:r + 1], post_var[:, r:r + 1], half[:, 0:1], ALU.pow
                                            ).then_inc(post_scale, 1)
                    pool.wait_ge(y_norm, T + 1)
                    tile = xt[:, bass.ds(T, 1), :].rearrange("p o e -> p (o e)")
                    nc.gpsimd.tensor_tensor(tile, tile, y_sb[:, r], ALU.add).then_inc(x1_ready, 1)
                if step == 7:
                    pool.wait_ge(post2_eps, T + 1)
                    nc.gpsimd.tensor_tensor(post_rstd[:, r:r + 1], post_var[:, r:r + 1], half[:, 0:1], ALU.pow
                                            ).then_inc(post2_scale, 1)

            def low_half(b, f, c):
                u = 2 * b + f
                if c % 5 in POOL_LOW:
                    pool.wait_ge(high_done, u * NC + c + 1)
                    s = half_slot(f, c)
                    nc.gpsimd.tensor_tensor(probsl[:, s], probs[:, c % 4], f32(probsh[:, s]), ALU.subtract
                                            ).then_inc(low_pool, 1)

            def add_v_parts(b, f, p):
                n = (2 * b + f) * NPAIR + p
                pool.wait_ge(o_copied, n + 2)
                wait(pool, attn_ready, n)
                nc.gpsimd.tensor_tensor(o_sum[:], o_raw[:, :, :, 0:HD], o_raw[:, :, :, HD:2 * HD], ALU.add
                                        ).then_inc(osum_ready, 1)

            def project_batch_norm(b):
                pool.wait_ge(ln1_eps, b + 1)
                nc.gpsimd.tensor_tensor(ln1_rstd[:], ln1_var[:], half[:], ALU.pow).then_inc(ln1_scale, 1)

            def slot(b, f, side_project, side_close, before):
                for pos in range(NC):
                    if pos == 0 and side_project is not None:
                        project_batch_norm(side_project)
                    if pos == 4 and before is not None:
                        add_v_parts(*before)
                    if pos > 5 and pos % 5 == 4:
                        add_v_parts(b, f, pos // 5 - 1)
                    if side_project is not None:
                        for i, s in project_steps(pos):
                            project(side_project, i, s)
                    if side_close is not None:
                        for i, s in close_steps(pos):
                            close(side_close, i, s)
                    low_half(b, f, pos)

            project_batch_norm(0)
            for i in range(QT):
                project(0, i, 5)
            slot(0, 0, None, None, None)
            with pool.Fori(0, BATCHES - 1) as b:
                slot(b, 1, b + 1, None, (b, 0, NPAIR - 1))
                slot(b + 1, 0, None, b, (b, 1, NPAIR - 1))
            slot(BATCHES - 1, 1, None, None, (BATCHES - 1, 0, NPAIR - 1))
            add_v_parts(BATCHES - 1, 1, NPAIR - 1)
            for pos in range(NC):
                for i, s in close_steps(pos):
                    close(BATCHES - 1, i, s)

            pool.wait_ge(gates_ready, TILES)

            def weights(ep, slot):
                e = 2 * ep + slot
                pool.wait_ge(w_load[slot], 32 * ep + 32)
                alone(pool)
                nc.gpsimd.tensor_copy(w13h[:, slot], w13f[:, slot]).then_inc(wh_made, 1)
                nc.gpsimd.tensor_copy(w2h[:, slot], w2f[:, slot]).then_inc(wh_made, 1)
                pool.wait_ge(wh_made, 2 * e + 2)
                nc.gpsimd.tensor_tensor(w13l[:, slot], w13f[:, slot], f32(w13h[:, slot]), ALU.subtract)
                nc.gpsimd.tensor_tensor(w2l[:, slot], w2f[:, slot], f32(w2h[:, slot]), ALU.subtract
                                        ).then_inc(w_split, 1)

            def hidden_low(ep, n):
                u = UNITS * ep + n
                pool.wait_ge(hidh_ready, u + 1)
                nc.gpsimd.tensor_tensor(hidl[:, n % 4], hid[:, n % 2], f32(hidh[:, n % 4]), ALU.subtract
                                        ).then_inc(hidl_ready, 1)

            weights(0, 0)
            weights(0, 1)
            hidden_low(0, 0)
            hidden_low(0, 1)
            with pool.Fori(0, EPAIRS - 1) as ep:
                for n in range(2, UNITS + 2):
                    hidden_low(ep + n // UNITS, n % UNITS)
                    if n == 5:
                        pool.wait_ge(down_psum, UNITS * ep + CHUNKS)
                        weights(ep + 1, 0)
                pool.wait_ge(down_psum, UNITS * ep + UNITS)
                weights(ep + 1, 1)
            for n in range(2, UNITS):
                hidden_low(EPAIRS - 1, n)

            for t in range(TILES):
                pool.wait_ge(fin_eps, t + 1)
                nc.gpsimd.tensor_tensor(fin_rstd[:, t:t + 1], fin_var[:, t:t + 1], half[:, 0:1], ALU.pow
                                        ).then_inc(fin_scale, 1)
                pool.wait_ge(fin_norm, t + 1)
                nc.gpsimd.tensor_tensor(ybuf[:, t, :], ybuf[:, t, :], xt[:, t, :], ALU.add
                                        ).then_inc(fin_ready, 1)

        @block.scalar
        def _(act):
            act.sem_inc(exp_done, 2)
            act.sem_inc(o_copied, 1)

            def project(b, i, step):
                t = b * QT + i
                if step == 2:
                    act.wait_ge(xnT_psum, t + 1)
                    wait(act, qkv_psum, t)
                    nc.scalar.copy(xnTh[:], bank[XT][:, 0:EMB].rearrange("p (c n) -> p c n", c=KC)
                                   ).then_inc(xnTh_ready, 1)
                if step == 4:
                    act.wait_ge(qkv_psum, t + 1)
                    if i == 0:
                        wait(act, vl_ready, 2 * b)
                    nc.scalar.copy(v_stage[:, i], bank[VB][:, 0:EMB].rearrange("p (h d) -> p h d", h=HEADS)
                                   ).then_inc(v_staged, 1)
                if step == 7:
                    act.wait_ge(qkT_psum, t + 1)
                    wait(act, s_spill, 32 * t)
                    nc.scalar.copy(qkTh[:], bank[SCORE[i % 2]][:, :].rearrange("p (w n) -> p w n", w=4)
                                   ).then_inc(qkTh_ready, 1)

            def cut_v(b, f):
                act.wait_ge(v_staged, QT * b + QT)
                if not isinstance(b, int):
                    act.wait_ge(pv_psum, 2 * (2 * b + f - 1) * NPAIR + 4)
                for h in range(2):
                    nc.scalar.copy(vs[:, f, :, :, 2 * h, 0:HD], v_stage[:, :, f * HALF + h:(f + 1) * HALF:2]
                                   ).then_inc(vh_ready, 1)

            def maxima_out(b, f):
                u = 2 * b + f
                act.wait_ge(maxT_psum, u + 1)
                wait(act, s_max_out, 16 * u)
                rows = slice(f * P // 2, (f + 1) * P // 2)
                nc.scalar.copy(maxT[rows], bank[SCORE[0]][rows, 0:P]).then_inc(maxT_ready, 1)

            def close(b, i, step):
                T, r = b * QT + i, i % 2
                if step == 2:
                    act.wait_ge(attnT_psum, T + 2)
                    nc.scalar.copy(attnTh[:, r], bank[QK][:, 0:EMB].rearrange("p (c n) -> p c n", c=KC)
                                   ).then_inc(attnTh_ready, 1)
                if step == 9:
                    act.wait_ge(xn2T_psum, T + 1)
                    xn2T = bank[XT][:, 0:EMB].rearrange("p (c n) -> p c n", c=KC)
                    nc.scalar.copy(xh_tile[:, r], xn2T).then_inc(xh_ready, 1)
                    nc.scalar.copy(x2T[:, :, bass.ds(T * P, P)], xn2T).then_inc(x2T_ready, 1)
                if step == 11:
                    act.wait_ge(router_psum, T + 1)
                    nc.scalar.copy(logits[:, r], bank[XT][:, EMB:EMB + EXPERTS]).then_inc(logits_ready, 1)
                if step == 13:
                    act.wait_ge(negtop_ready, T + 1)
                    nc.scalar.activation(expl[:, r], logits[:, r], ACTF.Exp, bias=negtop[:, r:r + 1]
                                         ).then_inc(expl_ready, 1)

            def exponentials(b, f, c):
                u = 2 * b + f
                n = u * NC + c
                act.wait_ge(weigh_psum, n + 1)
                by_pool = (c - 4) % 5 in POOL_LOW
                act.wait_ge(low_pool if by_pool else low_dve, low_count(u, c - 3, by_pool) + 4)
                nc.scalar.activation(probs[:, c % 4], bank[WEIGH[c % 2]][:, :], ACTF.Exp).then_inc(exp_done, 1)
                if c % 5 == 0:
                    act.wait_ge(pv_psum, 2 * (u * NPAIR + c // 5) + 2)
                if c % 5 == 3:
                    act.wait_ge(pv_psum, 2 * (u * NPAIR + c // 5) + 3)
                act.wait_ge(exp_done, n + 3)
                nc.scalar.copy(probsh[:, half_slot(f, c)], probs[:, c % 4]).then_inc(high_done, 1)

            def copy_transposed(b, f, p):
                n = (2 * b + f) * NPAIR + p
                act.wait_ge(pv_psum, 2 * n + 6)
                nc.scalar.copy(oT[0:2 * VW], bank[OB][0:2 * VW, :]).then_inc(oT_ready, 1)

            def copy_output(b, f, p):
                n = (2 * b + f) * NPAIR + p
                act.wait_ge(o_psum, n + 1)
                wait(act, osum_ready, n)
                wait(act, inv_ready, n)
                nc.scalar.copy(o_raw[:], bank[OB][:, :].rearrange("p (i n) -> p i n", i=QT)[:, :, 0:2 * VW].rearrange("p i (a v) -> p a i v", a=2)
                               ).then_inc(o_copied, 1)

            def slot(b, f, side_project, side_close, before):
                for pos in range(NC):
                    if side_project is None and f == 0 and pos == 4:
                        cut_v(b, 1)
                    exponentials(b, f, pos)
                    if pos == 1 and before is not None:
                        copy_transposed(*before)
                    if pos > 5 and pos % 5 == 1:
                        copy_transposed(b, f, pos // 5 - 1)
                    if pos == 3 and before is not None:
                        copy_output(*before)
                    if pos > 5 and pos % 5 == 3:
                        copy_output(b, f, pos // 5 - 1)
                    if side_project is not None:
                        for i, s in project_steps(pos):
                            project(side_project, i, s)
                        if pos == NC - 1:
                            cut_v(side_project, 0)
                    if side_close is not None:
                        for i, s in close_steps(pos):
                            close(side_close, i, s)
                    if side_project is None and f == 0 and pos == 16:
                        maxima_out(b, 1)
                    if side_project is not None and pos == 18:
                        maxima_out(side_project, 0)

            for pos in range(NC):
                for i, s in project_steps(pos):
                    project(0, i, s)
            cut_v(0, 0)
            maxima_out(0, 0)
            slot(0, 0, None, None, None)
            with act.Fori(0, BATCHES - 1) as b:
                slot(b, 1, b + 1, None, (b, 0, NPAIR - 1))
                slot(b + 1, 0, None, b, (b, 1, NPAIR - 1))
            slot(BATCHES - 1, 1, None, None, (BATCHES - 1, 0, NPAIR - 1))
            copy_transposed(BATCHES - 1, 1, NPAIR - 1)
            copy_output(BATCHES - 1, 1, NPAIR - 1)
            for pos in range(NC):
                for i, s in close_steps(pos):
                    close(BATCHES - 1, i, s)

            act.wait_ge(gates_ready, TILES)
            for c in range(KC):
                nc.scalar.copy(xh[:, c], x2T[:, c]).then_inc(xh_cut, 1)

            def unit(ep, n):
                u = UNITS * ep + n
                act.wait_ge(gu_psum, u + 1)
                nc.scalar.activation(silu[:, n % 2], bank[n % 2][0:FF, :], ACTF.Silu).then_inc(silu_ready, 1)
                act.wait_ge(hid_ready, u + 1)
                nc.scalar.copy(hidh[:, n % 4], hid[:, n % 2]).then_inc(hidh_ready, 1)

            with act.Fori(0, EPAIRS) as ep:
                for n in range(UNITS):
                    unit(ep, n)

        @block.vector
        def _(dve):
            dve.sem_inc(max_done, 2)
            dve.sem_inc(low_dve, 4)
            nc.vector.memset(half[:], -0.5).then_inc(s_prep, 1)
            dve.wait_ge(s_const, 16 * 6)
            nc.vector.tensor_copy(wqkvh[:], wqkv_f).then_inc(s_prep, 1)
            nc.vector.tensor_copy(woh[:], wo_f).then_inc(s_prep, 1)
            nc.vector.tensor_copy(wgh[:], wg_f).then_inc(s_prep, 1)
            nc.vector.tensor_copy(ident_b[:], ident_f[:]).then_inc(s_prep, 1)
            nc.vector.tensor_copy(mask_b[:], mask_f).then_inc(s_prep, 1)
            dve.wait_ge(s_prep, 6)
            nc.vector.tensor_tensor(wqkvl[:], wqkv_f, f32(wqkvh[:]), ALU.subtract).then_inc(s_prep, 1)
            nc.vector.tensor_tensor(wol[:], wo_f, f32(woh[:]), ALU.subtract).then_inc(s_prep, 1)
            nc.vector.tensor_tensor(wgl[:], wg_f, f32(wgh[:]), ALU.subtract).then_inc(s_prep, 1)

            def tile_of(buf, T):
                return buf[:, bass.ds(T, 1), :].rearrange("p o e -> p (o e)")

            def mean_var(n, stat, mv, var, src, s_bn, s_mean, s_eps):
                alone(dve)
                nc.vector.bn_stats(stat, src).then_inc(s_bn, 1)
                dve.wait_ge(s_bn, n + 1)
                alone(dve)
                nc.vector.bn_aggr(mv, stat).then_inc(s_mean, 1)
                dve.wait_ge(s_mean, n + 1)
                nc.vector.tensor_scalar(var, mv[:, 1:2], EPS, None, ALU.add).then_inc(s_eps, 1)

            def batch_norm_stats(b):
                dve.wait_ge(s_x, 16 * b + 16)
                alone(dve)
                for i in range(QT):
                    nc.vector.bn_stats(ln1_stat[:, i], tile_of(xt, b * QT + i)).then_inc(ln1_bn, 1)
                dve.wait_ge(ln1_bn, QT * b + QT)
                alone(dve)
                for i in range(QT):
                    nc.vector.bn_aggr(ln1_mv[:, i], ln1_stat[:, i]).then_inc(ln1_mean, 1)
                dve.wait_ge(ln1_mean, QT * b + QT)
                nc.vector.tensor_scalar(ln1_var[:], ln1_mv[:, :, 1], EPS, None, ALU.add).then_inc(ln1_eps, 1)

            def project(b, i, step):
                t = b * QT + i
                if step == 0:
                    if i == 0:
                        dve.wait_ge(ln1_scale, b + 1)
                    wait(dve, xnT_psum, t)
                    nc.vector.tensor_scalar(xn[:], tile_of(xt, t), ln1_mv[:, i, 0:1], ln1_rstd[:, i:i + 1],
                                            ALU.subtract, ALU.mult).then_inc(xn_ready, 1)
                if step == 3:
                    dve.wait_ge(xnTh_ready, t + 1)
                    nc.vector.tensor_tensor(xnTl[:], bank[XT][:, 0:EMB].rearrange("p (c n) -> p c n", c=KC),
                                            f32(xnTh[:]), ALU.subtract).then_inc(xnTl_ready, 1)
                if step == 4:
                    dve.wait_ge(qkv_psum, t + 1)
                    wait(dve, qkT_psum, t)
                    qk = bank[QK][:, :].rearrange("p (w h d) -> p w h d", w=2, h=HEADS)
                    cos = rope_sb[:, i, 0].unsqueeze(2)
                    sin = rope_sb[:, i, 1].unsqueeze(2)
                    nc.vector.tensor_tensor(rope_cos[:], qk, cos.broadcast_to([P, 2, HEADS, HD]), ALU.mult)
                    for o in range(2):
                        last = nc.vector.tensor_tensor(rope_sin[:, :, :, o::2], qk[:, :, :, 1 - o::2],
                                                       sin[:, :, :, o::2].broadcast_to([P, 2, HEADS, HD // 2]), ALU.mult)
                    last.then_inc(rope_parts, 1)
                if step == 7:
                    dve.wait_ge(qkTh_ready, t + 1)
                    wait(dve, s_spill, 32 * t)
                    nc.vector.tensor_tensor(qkTl[:], bank[SCORE[i % 2]][:, :].rearrange("p (w n) -> p w n", w=4),
                                            f32(qkTh[:]), ALU.subtract).then_inc(qkTl_ready, 1)

            def cut_v(b, f):
                dve.wait_ge(vh_ready, 2 * (2 * b + f) + 2)
                for h in range(2):
                    last = nc.vector.tensor_tensor(vs[:, f, :, :, 2 * h, HD:2 * HD],
                                                   v_stage[:, :, f * HALF + h:(f + 1) * HALF:2],
                                                   f32(vs[:, f, :, :, 2 * h, 0:HD]), ALU.subtract)
                last.then_inc(vl_ready, 1)

            def row_maxima(b, f, c):
                u = 2 * b + f
                dve.wait_ge(score_psum, u * NC + c + 1)
                if c == 0:
                    wait(dve, maxl_ready, u)
                places = PAIR_BANKS[c % 5]
                h0 = 2 * (c // 5)
                S = bank[SCORE[c % 2]]
                if len(places) == 2 and places[0][1] == places[1][1]:
                    i = places[0][1]
                    last = nc.vector.tensor_reduce(negmax[:, i, h0:h0 + 2], S[:, :].rearrange("p (a l) -> p a l", a=2),
                                                   AXX, ALU.max, negate=True)
                else:
                    for h, i, col in places:
                        last = nc.vector.tensor_reduce(negmax[:, i, h0 + h:h0 + h + 1], S[:, col:col + P * (i + 1)],
                                                       AXX, ALU.max, negate=True)
                last.then_inc(max_done, 1)

            def cut_maxima(b, f):
                u = 2 * b + f
                dve.wait_ge(max_done, u * NC + NC + 2)
                wait(dve, maxT_psum, u)
                nc.vector.tensor_copy(maxhl[:, f, :, 0, :].bitcast(F32R), negmax[:]).then_inc(maxh_ready, 1)
                dve.wait_ge(maxh_ready, u + 1)
                nc.vector.tensor_tensor(maxhl[:, f, :, 1, :], negmax[:], maxhl[:, f, :, 0, :], ALU.subtract
                                        ).then_inc(maxl_ready, 1)

            def low_half(b, f, c):
                u = 2 * b + f
                if c % 5 not in POOL_LOW:
                    dve.wait_ge(high_done, u * NC + c + 1)
                    s = half_slot(f, c)
                    nc.vector.tensor_tensor(probsl[:, s], probs[:, c % 4], f32(probsh[:, s]), ALU.subtract
                                            ).then_inc(low_dve, 1)

            def invert_sums(b, f, p):
                n = (2 * b + f) * NPAIR + p
                dve.wait_ge(o_copied, n + 2)
                wait(dve, attn_ready, n)
                nc.vector.reciprocal(o_inv[:], o_raw[:, :, :, 2 * HD]).then_inc(inv_ready, 1)

            def normalise(b, f, p):
                n = (2 * b + f) * NPAIR + p
                goal = attn[:, :, HALF + 2 * p:HALF + 2 * p + 2] if f == 1 else attn_first[:, :, 2 * p:2 * p + 2]
                dve.wait_ge(osum_ready, n + 1)
                dve.wait_ge(inv_ready, n + 1)
                nc.vector.tensor_tensor(goal.rearrange("p i a d -> p a i d"), o_sum[:],
                                        o_inv[:].unsqueeze(3).broadcast_to([P, 2, QT, HD]), ALU.mult
                                        ).then_inc(attn_ready, 1)

            def join_halves(b):
                dve.wait_ge(attn_ready, (2 * b + 1) * NPAIR)
                dve.wait_ge(attnT_psum, QT * b + 1)
                nc.vector.tensor_copy(attn[:, :, 0:HALF], attn_first[:]).then_inc(joined, 1)

            def close(b, i, step):
                T, r = b * QT + i, i % 2
                if step == 3:
                    dve.wait_ge(attnTh_ready, T + 1)
                    nc.vector.tensor_tensor(attnTl[:, r], bank[QK][:, 0:EMB].rearrange("p (c n) -> p c n", c=KC),
                                            f32(attnTh[:, r]), ALU.subtract).then_inc(attnTl_ready, 1)
                if step == 4:
                    dve.wait_ge(wo_psum, T + 1)
                    mean_var(T, post_stat[:, r], post_mv[:, r], post_var[:, r:r + 1], bank[VB][:, 0:EMB],
                             post_bn, post_mean, post_eps)
                if step == 5:
                    dve.wait_ge(post_scale, T + 1)
                    nc.vector.tensor_scalar(y_sb[:, r], bank[VB][:, 0:EMB], post_mv[:, r, 0:1], post_rstd[:, r:r + 1],
                                            ALU.subtract, ALU.mult).then_inc(y_norm, 1)
                if step == 6:
                    dve.wait_ge(x1_ready, T + 1)
                    mean_var(T, post_stat[:, r], post_mv[:, r], post_var[:, r:r + 1], tile_of(xt, T),
                             post2_bn, post2_mean, post2_eps)
                if step == 7:
                    dve.wait_ge(post2_scale, T + 1)
                    nc.vector.tensor_scalar(xn2[:, r], tile_of(xt, T), post_mv[:, r, 0:1], post_rstd[:, r:r + 1],
                                            ALU.subtract, ALU.mult).then_inc(xn2_ready, 1)
                if step == 9:
                    dve.wait_ge(xh_ready, T + 1)
                    dve.wait_ge(x2T_ready, T + 1)
                    nc.vector.tensor_tensor(xl_tile[:, r], bank[XT][:, 0:EMB].rearrange("p (c n) -> p c n", c=KC),
                                            f32(xh_tile[:, r]), ALU.subtract).then_inc(xl_ready, 1)
                if step == 12:
                    dve.wait_ge(logits_ready, T + 1)
                    alone(dve)
                    nc.vector.max(top[:, r], logits[:, r]).then_inc(top_ready, 1)
                    dve.wait_ge(top_ready, T + 1)
                    nc.vector.tensor_scalar(negtop[:, r:r + 1], top[:, r, 0:1], -1.0, None, ALU.mult
                                            ).then_inc(negtop_ready, 1)
                    nc.vector.match_replace(struck[:, r], top[:, r], logits[:, r], -3.0e38).then_inc(struck_ready, 1)
                    dve.wait_ge(struck_ready, T + 1)
                    nc.vector.tensor_tensor(chosen[:, r], struck[:, r], logits[:, r], ALU.not_equal
                                            ).then_inc(chosen_ready, 1)
                if step == 13:
                    dve.wait_ge(expl_ready, T + 1)
                    dve.wait_ge(chosen_ready, T + 1)
                    nc.vector.tensor_tensor(picked[:, r], expl[:, r], chosen[:, r], ALU.mult).then_inc(picked_ready, 1)
                    dve.wait_ge(picked_ready, T + 1)
                    nc.vector.reduce_sum(gsum[:, r:r + 1], picked[:, r], AXX).then_inc(gsum_ready, 1)
                    dve.wait_ge(gsum_ready, T + 1)
                    nc.vector.reciprocal(ginv[:, r:r + 1], gsum[:, r:r + 1]).then_inc(ginv_ready, 1)
                    dve.wait_ge(ginv_ready, T + 1)
                    nc.vector.tensor_scalar(tile_of(gates, T), picked[:, r], ginv[:, r:r + 1], None, ALU.mult
                                            ).then_inc(gates_ready, 1)

            def slot(b, f, side_project, side_close, before):
                for pos in range(NC):
                    if side_project is None and f == 0 and pos == 4:
                        cut_v(b, 1)
                    if pos == 0 and side_project is not None:
                        batch_norm_stats(side_project)
                    if pos == 4 and before is not None:
                        invert_sums(*before)
                        normalise(*before)
                        if f == 1:
                            join_halves(b)
                    if pos > 5 and pos % 5 == 4:
                        invert_sums(b, f, pos // 5 - 1)
                        normalise(b, f, pos // 5 - 1)
                    if side_project is not None:
                        for i, s in project_steps(pos):
                            project(side_project, i, s)
                        if pos == NC - 1:
                            cut_v(side_project, 0)
                        for c in late_scores(pos):
                            row_maxima(side_project, 0, c)
                        if pos == 17:
                            cut_maxima(side_project, 0)
                    elif f == 0:
                        for c in early_scores(pos):
                            row_maxima(b, 1, c)
                        if pos == 15:
                            cut_maxima(b, 1)
                    if side_close is not None:
                        for i, s in close_steps(pos):
                            close(side_close, i, s)
                    low_half(b, f, pos)

            batch_norm_stats(0)
            for pos in range(NC):
                for i, s in project_steps(pos):
                    project(0, i, s)
            cut_v(0, 0)
            for c in range(NC):
                row_maxima(0, 0, c)
            cut_maxima(0, 0)
            slot(0, 0, None, None, None)
            with dve.Fori(0, BATCHES - 1) as b:
                slot(b, 1, b + 1, None, (b, 0, NPAIR - 1))
                slot(b + 1, 0, None, b, (b, 1, NPAIR - 1))
            slot(BATCHES - 1, 1, None, None, (BATCHES - 1, 0, NPAIR - 1))
            invert_sums(BATCHES - 1, 1, NPAIR - 1)
            normalise(BATCHES - 1, 1, NPAIR - 1)
            for pos in range(NC):
                for i, s in close_steps(pos):
                    close(BATCHES - 1, i, s)

            dve.wait_ge(gates_ready, TILES)
            for c in range(KC):
                dve.wait_ge(xh_cut, c + 1)
                nc.vector.tensor_tensor(xl[:, c], x2T[:, c], f32(xh[:, c]), ALU.subtract).then_inc(xl_cut, 1)
            for c in range(2):
                nc.vector.memset(acc[:, c * TILES // 2:(c + 1) * TILES // 2], 0.0).then_inc(acc_done, 1)

            def hidden(ep, n, first=False):
                u = UNITS * ep + n
                dve.wait_ge(silu_ready, u + 1)
                if not first:
                    dve.wait_ge(hidl_ready, u - 1)
                nc.vector.tensor_tensor(hid[:, n % 2], silu[:, n % 2], bank[2 + n % 2][0:FF, :], ALU.mult
                                        ).then_inc(hid_ready, 1)

            def gather_up(ep, n):
                u = UNITS * ep + n
                e = 2 * ep + n // CHUNKS
                c = n % CHUNKS
                dve.wait_ge(down_psum, u + 1)
                dve.wait_ge(acc_done, u + 2)
                for k in range(4):
                    t = 4 * c + k
                    r = nc.vector.scalar_tensor_tensor(
                        acc[:, t, :], bank[4 + 2 * (n % 2) + k // 2][:, (k % 2) * EMB:(k % 2 + 1) * EMB],
                        gates[:, t, bass.ds(e, 1)], acc[:, t, :], ALU.mult, ALU.add)
                r.then_inc(acc_done, 1)

            hidden(0, 0, first=True)
            hidden(0, 1, first=True)
            with dve.Fori(0, EPAIRS - 1) as ep:
                for n in range(2, UNITS + 2):
                    hidden(ep + n // UNITS, n % UNITS)
                    gather_up(ep, n - 2)
            ep = EPAIRS - 1
            for n in range(2, UNITS + 2):
                if n < UNITS:
                    hidden(ep, n)
                gather_up(ep, n - 2)

            for t in range(TILES):
                dve.wait_ge(acc_done, UNITS * EPAIRS + 2)
                mean_var(t, fin_stat[:, t], fin_mv[:, t], fin_var[:, t:t + 1], acc[:, t, :], fin_bn, fin_mean, fin_eps)
            for t in range(TILES):
                dve.wait_ge(fin_scale, t + 1)
                nc.vector.tensor_scalar(ybuf[:, t, :], acc[:, t, :], fin_mv[:, t, 0:1], fin_rstd[:, t:t + 1],
                                        ALU.subtract, ALU.mult).then_inc(fin_norm, 1)

        @block.tensor
        def _(pe):
            pe.sem_inc(pv_psum, 4)
            pe.sem_inc(attnT_psum, 1)
            pe.wait_ge(s_const, 16 * 6)
            pe.wait_ge(s_prep, 9)
            pe.wait_ge(s_ones, 7)

            def transpose2(dst, src):
                for c in range(KC):
                    last = nc.tensor.matmul(dst[:, c * P:(c + 1) * P], src[:, c * P:(c + 1) * P], ident_f[:],
                                            is_transpose=True, start=True, stop=True)
                return last

            def three_passes(dst, parts):
                products = [p for ah, al, bh, bl in parts for p in ((ah, bh), (ah, bl), (al, bh))]
                for k, (a, w) in enumerate(products):
                    last = nc.tensor.matmul(dst, a, w, start=(k == 0), stop=(k == len(products) - 1))
                return last

            def project(b, i, step):
                t = b * QT + i
                if step == 1:
                    pe.wait_ge(xn_ready, t + 1)
                    wait(pe, xnTl_ready, t)
                    transpose2(bank[XT], xn).then_inc(xnT_psum, 1)
                if step == 3:
                    pe.wait_ge(xnTl_ready, t + 1)
                    wait(pe, rope_parts, t)
                    wait(pe, v_staged, t)
                    three_passes(bank[QK][:, :], [(xnTh[:, c], xnTl[:, c], wqkvh[:, c, 0:2 * EMB], wqkvl[:, c, 0:2 * EMB])
                                                  for c in range(KC)])
                    three_passes(bank[VB][:, 0:EMB], [(xnTh[:, c], xnTl[:, c], wqkvh[:, c, 2 * EMB:], wqkvl[:, c, 2 * EMB:])
                                                      for c in range(KC)]).then_inc(qkv_psum, 1)
                if step == 6:
                    pe.wait_ge(rope_done, t + 1)
                    wait(pe, qkTl_ready, t)
                    for w in range(4):
                        last = nc.tensor.matmul(
                            bank[SCORE[i % 2]][:, w * P:(w + 1) * P],
                            rope_cos[:, w // 2, (w % 2) * HALF:(w % 2 + 1) * HALF].rearrange("p h d -> p (h d)"),
                            ident_f[:], is_transpose=True, start=True, stop=True)
                    last.then_inc(qkT_psum, 1)

            def scores(b, f, c):
                u = 2 * b + f
                if c == 0:
                    pe.wait_ge(s_load, 144 * u + 144)
                    wait(pe, maxT_ready, u)
                pe.wait_ge(max_done, u * NC + c + 1)
                for h, i, col in PAIR_BANKS[c % 5]:
                    a = 2 * (c // 5) + h
                    L = P * (i + 1)
                    S = bank[SCORE[c % 2]]
                    nc.tensor.matmul(S[:, col + L - P:col + L], ident_b[:], mask_b[:],
                                     start=True, stop=False, skip_group_check=True)
                    last = nc.tensor.matmul(S[:, col:col + L], qs[f][:, a, i * P:(i + 1) * P], ks[f][:, a, 0:L],
                                            start=False, stop=True, skip_group_check=True)
                last.then_inc(score_psum, 1)

            def transpose_maxima(b, f):
                u = 2 * b + f
                pe.wait_ge(maxl_ready, u + 1)
                wait(pe, maxT_ready, u)
                nc.tensor.matmul(bank[SCORE[0]][:, 0:P],
                                 maxhl[:].rearrange("p f i c a -> p (f i c a)"), ident_f[:],
                                 is_transpose=True, start=True, stop=True).then_inc(maxT_psum, 1)

            def weigh(b, f, c):
                u = 2 * b + f
                if c == 0:
                    pe.wait_ge(s_max_in, 64 * u + 64)
                pe.wait_ge(exp_done, u * NC + c + 1)
                for h, r, col in PAIR_BANKS[c % 5]:
                    a = 2 * (c // 5) + h
                    j, N = QT - 1 - r, P * (r + 1)
                    S = bank[WEIGH[c % 2]]
                    nc.tensor.matmul(S[:, col:col + P], mask_b[:], ident_b[:],
                                     start=True, stop=False, skip_group_check=True)
                    last = nc.tensor.matmul(S[:, col:col + N], ks[f][:, a, j * P:(j + 1) * P], qs[f][:, a, j * P:],
                                            start=False, stop=True, skip_group_check=True)
                last.then_inc(weigh_psum, 1)

            def weigh_values(b, f, p, h):
                u = 2 * b + f
                n = u * NPAIR + p
                if h == 0:
                    if p == 0:
                        pe.wait_ge(vl_ready, u + 1)
                    pe.wait_ge(o_copied, n + 1)
                pe.wait_ge(low_pool, low_count(u, 5 * p + 3 + 2 * h, True) + 4)
                pe.wait_ge(low_dve, low_count(u, 5 * p + 3 + 2 * h, False) + 4)
                for j in range(QT):
                    w, col = KPLACE[(h, j)]
                    s = half_slot(f, 5 * p + w)
                    for pr in (probsh, probsl):
                        last = nc.tensor.matmul(
                            bank[OB][0:2 * VW, j * P:],
                            vs[:, f, j, p, h:h + 2].rearrange("p a v -> p (a v)"), pr[:, s, col:col + (QT - j) * P], start=(h == 0 and j == 0 and pr is probsh),
                            stop=(h == 1 and j == QT - 1 and pr is probsl), skip_group_check=True)
                last.then_inc(pv_psum, 1)

            def transpose_output(b, f, p):
                n = (2 * b + f) * NPAIR + p
                pe.wait_ge(oT_ready, n + 1)
                for i in range(QT):
                    last = nc.tensor.matmul(bank[OB][:, i * P:(i + 1) * P], oT[:, i * P:(i + 1) * P], ident_f[:],
                                            is_transpose=True, start=True, stop=True)
                last.then_inc(o_psum, 1)

            def close(b, i, step):
                T, r = b * QT + i, i % 2
                if step == 1:
                    pe.wait_ge(attn_ready, 2 * NPAIR * (b + 1))
                    pe.wait_ge(joined, b + 1)
                    if i > 0:
                        pe.wait_ge(attnTl_ready, T)
                    transpose2(bank[QK], attn[:, i].rearrange("p h d -> p (h d)")).then_inc(attnT_psum, 1)
                if step == 3:
                    pe.wait_ge(attnTl_ready, T + 1)
                    if i > 0:
                        pe.wait_ge(y_norm, T)
                    three_passes(bank[VB][:, 0:EMB], [(attnTh[:, r, c], attnTl[:, r, c], woh[:, c], wol[:, c])
                                                      for c in range(KC)]).then_inc(wo_psum, 1)
                if step == 8:
                    pe.wait_ge(xn2_ready, T + 1)
                    if i > 0:
                        pe.wait_ge(logits_ready, T)
                    transpose2(bank[XT][:, 0:EMB], xn2[:, r]).then_inc(xn2T_psum, 1)
                if step == 10:
                    pe.wait_ge(xl_ready, T + 1)
                    three_passes(bank[XT][:, EMB:EMB + EXPERTS], [(xh_tile[:, r, c], xl_tile[:, r, c], wgh[:, c], wgl[:, c])
                                                                  for c in range(KC)]).then_inc(router_psum, 1)

            def slot(b, f, side_project, side_close, before):
                weigh(b, f, 0)
                for pos in range(NC):
                    if pos + 1 < NC:
                        weigh(b, f, pos + 1)
                    if pos == 0 and before is not None:
                        weigh_values(*before, 1)
                    if pos == 2 and before is not None:
                        transpose_output(*before)
                    if pos % 5 == 4:
                        weigh_values(b, f, pos // 5, 0)
                    if pos >= 5 and pos % 5 == 0:
                        weigh_values(b, f, pos // 5 - 1, 1)
                    if pos >= 5 and pos % 5 == 2:
                        transpose_output(b, f, pos // 5 - 1)
                    if side_project is not None:
                        for i, s in project_steps(pos):
                            project(side_project, i, s)
                        for c in late_scores(pos):
                            scores(side_project, 0, c)
                        if pos == 18:
                            transpose_maxima(side_project, 0)
                    elif f == 0:
                        for c in early_scores(pos):
                            scores(b, 1, c)
                        if pos == 16:
                            transpose_maxima(b, 1)
                    if side_close is not None:
                        for i, s in close_steps(pos):
                            close(side_close, i, s)

            for pos in range(NC):
                for i, s in project_steps(pos):
                    project(0, i, s)
            for c in range(NC):
                scores(0, 0, c)
            transpose_maxima(0, 0)
            slot(0, 0, None, None, None)
            with pe.Fori(0, BATCHES - 1) as b:
                slot(b, 1, b + 1, None, (b, 0, NPAIR - 1))
                slot(b + 1, 0, None, b, (b, 1, NPAIR - 1))
            slot(BATCHES - 1, 1, None, None, (BATCHES - 1, 0, NPAIR - 1))
            weigh_values(BATCHES - 1, 1, NPAIR - 1, 1)
            transpose_output(BATCHES - 1, 1, NPAIR - 1)
            for pos in range(NC):
                for i, s in close_steps(pos):
                    close(BATCHES - 1, i, s)

            def gate_up(ep, n, first=False):
                u = UNITS * ep + n
                slot, c = n // CHUNKS, n % CHUNKS
                if c == 0:
                    pe.wait_ge(w_split, 2 * ep + slot + 1)
                if not first:
                    pe.wait_ge(hid_ready, u - 1)
                for dst, f0 in ((bank[n % 2], 0), (bank[2 + n % 2], FF)):
                    k = 0
                    for kc in range(KC):
                        for w, xx in ((w13h, xh), (w13h, xl), (w13l, xh)):
                            r = nc.tensor.matmul(dst[0:FF, :], w[:, slot, kc, f0:f0 + FF],
                                                 xx[:, kc, c * 512:(c + 1) * 512], start=(k == 0), stop=(k == 5))
                            k += 1
                r.then_inc(gu_psum, 1)

            def down(ep, n):
                u = UNITS * ep + n
                slot = n // CHUNKS
                pe.wait_ge(hidh_ready, u + 1)
                pe.wait_ge(hidl_ready, u + 1)
                pe.wait_ge(acc_done, u + 1)
                for k in range(4):
                    dst = bank[4 + 2 * (n % 2) + k // 2][:, (k % 2) * EMB:(k % 2 + 1) * EMB]
                    for m, (hh, w) in enumerate(((hidh, w2h), (hidh, w2l), (hidl, w2h))):
                        r = nc.tensor.matmul(dst, hh[:, n % 4, k * P:(k + 1) * P], w[:, slot, :],
                                             start=(m == 0), stop=(m == 2))
                r.then_inc(down_psum, 1)

            pe.wait_ge(gates_ready, TILES)
            pe.wait_ge(xl_cut, KC)
            gate_up(0, 0, first=True)
            gate_up(0, 1, first=True)
            with pe.Fori(0, EPAIRS - 1) as ep:
                for n in range(2, UNITS + 2):
                    gate_up(ep + n // UNITS, n % UNITS)
                    down(ep, n - 2)
            ep = EPAIRS - 1
            for n in range(2, UNITS + 2):
                if n < UNITS:
                    gate_up(ep, n)
                down(ep, n - 2)


_INS = ['L0_attn_x', 'L0_attn_Wqkv', 'L0_attn_Wo', 'L0_ffn_wg', 'L0_ffn_w1', 'L0_ffn_v1', 'L0_ffn_w2']


def kernel(**inputs):
    import numpy as np
    import concourse.bacc as bacc
    from concourse import mybir as mb
    from concourse.bass_utils import run_bass_kernel_spmd

    x, wqkv, wo, wg, w1, v1, w2 = (np.ascontiguousarray(inputs[n]) for n in _INS)
    f = np.float32
    inv = (f(1.0) / np.power(f(10000.0), f(2.0) * np.arange(HD // 2, dtype=f) / f(HD))).astype(f)
    angle = np.outer(np.arange(SEQ, dtype=f), inv).astype(f)
    cos, sin = np.cos(angle).astype(f), np.sin(angle).astype(f)
    table = np.stack([np.repeat(cos, 2, axis=1), np.stack([-sin, sin], axis=2).reshape(SEQ, HD)], axis=1)
    rope = np.ascontiguousarray(np.stack([table * f(0.25), table], axis=2))
    arrays = {
        "x": x, "wqkv": wqkv, "wo": wo,
        "wgT": np.ascontiguousarray(wg.T),
        "w13": np.ascontiguousarray(np.concatenate([w1, v1], axis=2)),
        "w2": w2,
        "ident": np.eye(P, dtype=f),
        "mask": np.triu(np.full((P, P), -1e30, dtype=f), 1),
        "rope": rope,
    }
    nc = bacc.Bacc("TRN2", target_bir_lowering=False, num_devices=1)
    args = [nc.dram_tensor(n, a.shape, mb.dt.from_np(a.dtype), kind="ExternalInput").ap() for n, a in arrays.items()]
    args.append(nc.dram_tensor("out", (BATCHES, SEQ, EMB), mb.dt.float32, kind="ExternalOutput").ap())
    build(nc, *args)
    r = run_bass_kernel_spmd(nc, [arrays], core_ids=[0])
    return r.results[0]["out"]
```

```python
import concourse.bass as bass
from concourse import mybir
from contextlib import ExitStack

F32 = mybir.dt.float32
F32R = mybir.dt.float32r
BF16 = mybir.dt.bfloat16
ACTF = mybir.ActivationFunctionType
ALU = mybir.AluOpType
AXX = mybir.AxisListType.X

P = 128
BATCHES, SEQ, EMB = 4, 512, 256
TOKENS = BATCHES * SEQ
TILES = TOKENS // P
QT = SEQ // P
KC = EMB // P
HEADS, HD = 16, 16
HALF = HEADS // 2
LOADS = 16 * 9
ROWS = 4 * HD + 2
VW = HD + 1
EXPERTS, TOPK, FF = 32, 8, 96
CHUNKS = TOKENS // 512
EPS = 1e-5

PAIR_BANKS = [[(0, 3, 0)], [(0, 2, 0), (0, 0, 384)], [(0, 1, 0), (1, 1, 256)], [(1, 3, 0)], [(1, 2, 0), (1, 0, 384)]]
NPAIR = HALF // 2
NC = len(PAIR_BANKS) * NPAIR
KPLACE = {(h, 3 - r): (w, col) for w, bank in enumerate(PAIR_BANKS) for h, r, col in bank}
RING = 2 * len(PAIR_BANKS)
CLOSE_AT = {1: 0, 2: 0, 3: 1, 4: 1, 5: 2, 6: 3, 7: 4, 8: 5, 9: 5, 10: 6, 11: 7, 12: 7, 13: 8}
PROJECT_AT = {0: 0, 1: 0, 2: 1, 3: 1, 4: 2, 5: 3, 6: 3, 7: 4}


def close_steps(pos):
    return [(i, s) for i in range(QT) for s, at in CLOSE_AT.items() if 5 + 2 * i + at == pos]


def project_steps(pos):
    return [(i, s) for i in range(QT) for s, at in PROJECT_AT.items() if 1 + 2 * i + at == pos]


def early_scores(pos):
    return [c for c in range(NC) if 4 + c * 12 // NC == pos]


def late_scores(pos):
    return [c for c in range(NC) if 13 + c * 5 // NC == pos]


def wait(engine, sem, value):
    if not isinstance(value, int) or value > 0:
        engine.wait_ge(sem, value)


def build(nc, x, wqkv, wo, wgT, w13, w2, ident, mask, rope, out):
    ctx = ExitStack()
    with ctx:
        def sb(name, shape, dt=F32):
            return ctx.enter_context(nc.sbuf_tensor(name, shape, dt))

        def sem(name):
            return ctx.enter_context(nc.semaphore(name))

        def f32(ap):
            return ap.bitcast(F32)

        qk_dram = nc.dram_tensor("qk_dram", (2, P, 4, SEQ), F32).ap()
        max_dram = nc.dram_tensor("max_dram", (2, QT, 2, HALF, P), F32).ap()

        xt = sb("xt", [P, TILES, EMB])
        x2T = sb("x2T", [P, KC, TOKENS])
        gates = sb("gates", [P, TILES, EXPERTS])
        half = sb("half", [P, QT])

        ph1 = ExitStack()
        ph1.__enter__()

        def sb1(name, shape, dt=F32):
            return ph1.enter_context(nc.sbuf_tensor(name, shape, dt))

        ident_f = sb1("ident_f", [P, P])
        ident_b = sb1("ident_b", [P, P], BF16)
        mask_b = sb1("mask_b", [P, P], BF16)
        wqkv_sb = sb1("wqkv_sb", [P, KC, 3 * EMB])
        wo_sb = sb1("wo_sb", [P, KC, EMB])
        wg_sb = sb1("wg_sb", [P, KC, EXPERTS])
        rope_sb = sb1("rope_sb", [P, QT, 2, 2, HD])
        ln1_stat = sb1("ln1_stat", [P, QT, 6])
        ln1_mv = sb1("ln1_mv", [P, QT, 2])
        ln1_var = sb1("ln1_var", [P, QT])
        ln1_rstd = sb1("ln1_rstd", [P, QT])
        xn = sb1("xn", [P, EMB])
        xnT = sb1("xnT", [P, KC, P])
        rope_cos = sb1("rope_cos", [P, 2, HEADS, HD])
        rope_sin = sb1("rope_sin", [P, 2, HEADS, HD])
        qkTh = sb1("qkTh", [P, 4, P], F32R)
        qkTl = sb1("qkTl", [P, 4, P], F32R)
        v_stage = sb1("v_stage", [P, QT, HEADS, HD])
        vs = sb1("vs", [P, 2, QT, NPAIR, 3, VW])
        qs = [sb1(f"qs{f}", [ROWS, HALF, SEQ], F32R) for f in range(2)]
        ks = [sb1(f"ks{f}", [ROWS, HALF, SEQ], F32R) for f in range(2)]
        probs = sb1("probs", [P, RING, 512])
        mask_f = v_stage[:, 1].rearrange("p h d -> p (h d)")[:, 0:P]
        negmax = sb1("negmax", [P, QT, HALF])
        maxhl = sb1("maxhl", [P, 2, QT, 2, HALF])
        maxT = sb1("maxT", [P, P])
        oT = sb1("oT", [P, SEQ])
        zeros = oT[P - 2:P]
        o_inv = sb1("o_inv", [P, 2, QT])
        attn_first = sb1("attn_first", [P, QT, HALF, HD])
        attn = sb1("attn", [P, QT, HEADS, HD])
        attnT = sb1("attnT", [P, 2, KC, P])
        y_sb = sb1("y_sb", [P, 2, EMB])
        xn2 = y_sb
        post_stat = sb1("post_stat", [P, 2, 6])
        post_mv = sb1("post_mv", [P, 2, 2])
        post_var = sb1("post_var", [P, 2])
        post_rstd = sb1("post_rstd", [P, 2])
        x2T_tile = sb1("x2T_tile", [P, 2, KC, P])
        logits = sb1("logits", [P, 2, EXPERTS])
        top = sb1("top", [P, 2, TOPK])
        negtop = sb1("negtop", [P, 2])
        struck = sb1("struck", [P, 2, EXPERTS])
        chosen = sb1("chosen", [P, 2, EXPERTS])
        expl = sb1("expl", [P, 2, EXPERTS])
        picked = sb1("picked", [P, 2, EXPERTS])
        gsum = sb1("gsum", [P, 2])
        ginv = sb1("ginv", [P, 2])
        ph1.close()

        xh = sb("xh", [P, KC, TOKENS], F32R)
        xl = sb("xl", [P, KC, TOKENS], F32R)
        acc = sb("acc", [P, TILES, EMB])
        w13f = sb("w13f", [P, 2, KC, 2 * FF])
        w2f = sb("w2f", [FF, 2, EMB])
        w13h = sb("w13h", [P, 2, KC, 2 * FF], F32R)
        w13l = sb("w13l", [P, 2, KC, 2 * FF], F32R)
        w2h = sb("w2h", [FF, 2, EMB], F32R)
        w2l = sb("w2l", [FF, 2, EMB], F32R)
        silu = sb("silu", [FF, 2, 512])
        hid = sb("hid", [FF, 2, 512])
        hidh = sb("hidh", [FF, 4, 512], F32R)
        hidl = sb("hidl", [FF, 4, 512], F32R)
        fin_stat = sb("fin_stat", [P, TILES, 6])
        fin_mv = sb("fin_mv", [P, TILES, 2])
        fin_var = sb("fin_var", [P, TILES])
        fin_rstd = sb("fin_rstd", [P, TILES])
        ybuf = sb("ybuf", [P, TILES, EMB])

        bank = [ctx.enter_context(nc.psum_tensor(f"bank{n}", [P, 512], F32)) for n in range(8)]
        SCORE, WEIGH, OB, QK, XT, VB = (0, 1), (2, 3), 4, 5, 6, 7

        s_const = sem("s_const")
        s_x = sem("s_x")
        s_prep = sem("s_prep")
        s_ones = sem("s_ones")
        ln1_bn = sem("ln1_bn"); ln1_mean = sem("ln1_mean"); ln1_eps = sem("ln1_eps")
        ln1_scale = sem("ln1_scale")
        xn_ready = sem("xn_ready")
        xnT_psum = sem("xnT_psum")
        xnT_ready = sem("xnT_ready")
        qkv_psum = sem("qkv_psum")
        v_staged = sem("v_staged")
        rope_parts = sem("rope_parts")
        rope_done = sem("rope_done")
        qkT_psum = sem("qkT_psum")
        qkTh_ready = sem("qkTh_ready")
        qkTl_ready = sem("qkTl_ready")
        s_spill = sem("s_spill")
        s_load = sem("s_load")
        v_ready = sem("v_ready")
        score_psum = sem("score_psum")
        max_done = sem("max_done")
        maxh_ready = sem("maxh_ready"); maxl_ready = sem("maxl_ready")
        maxT_psum = sem("maxT_psum")
        maxT_ready = sem("maxT_ready")
        s_max_out = sem("s_max_out")
        s_max_in = sem("s_max_in")
        weigh_psum = sem("weigh_psum")
        exp_done = sem("exp_done")
        pv_psum = sem("pv_psum")
        oT_ready = sem("oT_ready")
        o_psum = sem("o_psum")
        inv_ready = sem("inv_ready")
        attn_ready = sem("attn_ready")
        joined = sem("joined")
        attnT_psum = sem("attnT_psum")
        attnT_ready = sem("attnT_ready")
        wo_psum = sem("wo_psum")
        post_bn = sem("post_bn"); post_mean = sem("post_mean"); post_eps = sem("post_eps")
        post2_bn = sem("post2_bn"); post2_mean = sem("post2_mean"); post2_eps = sem("post2_eps")
        post_scale = sem("post_scale"); post2_scale = sem("post2_scale")
        y_norm = sem("y_norm")
        x1_ready = sem("x1_ready")
        xn2_ready = sem("xn2_ready")
        xn2T_psum = sem("xn2T_psum")
        x2T_ready = sem("x2T_ready")
        router_psum = sem("router_psum")
        logits_ready = sem("logits_ready")
        top_ready = sem("top_ready"); negtop_ready = sem("negtop_ready")
        struck_ready = sem("struck_ready"); chosen_ready = sem("chosen_ready")
        expl_ready = sem("expl_ready")
        picked_ready = sem("picked_ready"); gsum_ready = sem("gsum_ready")
        ginv_ready = sem("ginv_ready"); gates_ready = sem("gates_ready")
        xh_cut = sem("xh_cut")
        xl_cut = sem("xl_cut")
        w_load = [sem("w_load0"), sem("w_load1")]
        w_split = sem("w_split")
        wh_made = sem("wh_made")
        gu_psum = sem("gu_psum")
        silu_ready = sem("silu_ready")
        hid_ready = sem("hid_ready")
        hidh_ready = sem("hidh_ready")
        hidl_ready = sem("hidl_ready")
        down_psum = sem("down_psum")
        acc_done = sem("acc_done")
        fin_bn = sem("fin_bn"); fin_mean = sem("fin_mean"); fin_eps = sem("fin_eps")
        fin_scale = sem("fin_scale"); fin_norm = sem("fin_norm"); fin_ready = sem("fin_ready")
        s_out = sem("s_out")
        s_spare = sem("s_spare")

        block = ctx.enter_context(nc.Block())
        UNITS = 2 * CHUNKS
        EPAIRS = EXPERTS // 2

        def alone(engine):
            engine.sem_inc(s_spare, 1)

        @block.sync
        def _(sp):
            sp.dma_start(xt[:, 0:QT, :], x[0].rearrange("(t p) e -> p t e", p=P)).then_inc(s_x, 16)
            sp.dma_start(wqkv_sb[:], wqkv.rearrange("(c p) n -> p c n", p=P)).then_inc(s_const, 16)
            sp.dma_start(ident_f[:], ident).then_inc(s_const, 16)
            sp.dma_start(rope_sb[:], rope.rearrange("(t p) a b d -> p t a b d", p=P)).then_inc(s_const, 16)
            sp.dma_start(mask_f, mask).then_inc(s_const, 16)
            sp.dma_start(wo_sb[:], wo.rearrange("(c p) n -> p c n", p=P)).then_inc(s_const, 16)
            sp.dma_start(wg_sb[:], wgT.rearrange("(c p) n -> p c n", p=P)).then_inc(s_const, 16)
            for b in range(1, BATCHES):
                sp.wait_ge(s_x, 16 * b)
                sp.dma_start(xt[:, b * QT:(b + 1) * QT, :],
                             x[b].rearrange("(t p) e -> p t e", p=P)).then_inc(s_x, 16)
            sp.wait_ge(s_ones, 7)

            def spill(b):
                for i in range(QT):
                    t = QT * b + i
                    for c, part, ready in ((0, qkTh, qkTh_ready), (1, qkTl, qkTl_ready)):
                        sp.wait_ge(ready, t + 1)
                        alone(sp)
                        sp.dma_start(qk_dram[c, :, :, i * P:(i + 1) * P], f32(part[:])).then_inc(s_spill, 16)
                    sp.wait_ge(s_spill, 32 * t + 32)
                    alone(sp)

            def load_stacks(b, f):
                u = 2 * b + f
                wait(sp, weigh_psum, (u - 2) * NC + NC)
                alone(sp)
                sp.dma_start(f32(qs[f][4 * HD:ROWS]), zeros.unsqueeze(1).broadcast_to([2, HALF, SEQ])
                             ).then_inc(s_load, 16)
                for stack, w, cuts in ((qs[f], f, (0, 1, 0, 1)), (ks[f], 2 + f, (0, 0, 1, 1))):
                    for r, c in enumerate(cuts):
                        sp.dma_start(f32(stack[r * HD:(r + 1) * HD]),
                                     qk_dram[c, :, w, :].rearrange("(a d) t -> d a t", d=HD)).then_inc(s_load, 16)
                sp.wait_ge(s_load, LOADS * u + LOADS)
                alone(sp)

            def load_maxima(b, f):
                u = 2 * b + f
                sp.wait_ge(maxT_ready, u + 1)
                alone(sp)
                sp.dma_start(max_dram[f].rearrange("i c a t -> (i c a) t"), maxT[f * P // 2:(f + 1) * P // 2]).then_inc(s_max_out, 16)
                sp.wait_ge(s_max_out, 16 * u + 16)
                alone(sp)
                sp.dma_start(f32(qs[f][4 * HD:ROWS]).rearrange("c a (i t) -> c a i t", i=QT),
                             max_dram[f].rearrange("i c a t -> c a i t")).then_inc(s_max_in, 16)
                sp.wait_ge(s_max_in, 16 * u + 16)
                alone(sp)

            spill(0)
            load_stacks(0, 0)
            load_maxima(0, 0)
            load_stacks(0, 1)
            load_maxima(0, 1)
            with sp.Fori(0, BATCHES - 1) as b:
                spill(b + 1)
                for f in range(2):
                    load_stacks(b + 1, f)
                    load_maxima(b + 1, f)

            sp.wait_ge(gates_ready, TILES)

            def load_expert(e, slot):
                sp.dma_start(w13f[:, slot], w13[bass.ds(e, 1)].rearrange("o (c p) n -> p (o c) n", p=P)
                             ).then_inc(w_load[slot], 16)
                sp.dma_start(w2f[:, slot], w2[bass.ds(e, 1)].rearrange("o f n -> f (o n)")
                             ).then_inc(w_load[slot], 16)

            load_expert(0, 0)
            load_expert(1, 1)
            with sp.Fori(0, EPAIRS - 1) as ep:
                for slot in range(2):
                    sp.wait_ge(w_split, 2 * ep + slot + 1)
                    load_expert(2 * ep + 2 + slot, slot)

            for t in range(TILES):
                sp.wait_ge(fin_ready, t + 1)
                sp.dma_start(out[t // QT, (t % QT) * P:(t % QT + 1) * P, :], ybuf[:, t, :]).then_inc(s_out, 16)
            sp.wait_ge(s_out, 16 * TILES)


        @block.gpsimd
        def _(pool):
            for k, (buffer, value) in enumerate((
                    (maxhl[:], 0.0), (oT[:], 0.0), (f32(ks[0][4 * HD:ROWS]), 1.0), (f32(ks[1][4 * HD:ROWS]), 1.0),
                    (vs[:], 0.0), (vs[:, 0, :, :, 0::2, HD], 1.0), (vs[:, 1, :, :, 0::2, HD], 1.0))):
                if k:
                    pool.wait_ge(s_ones, k)
                nc.gpsimd.memset(buffer, value).then_inc(s_ones, 1)
            pool.wait_ge(s_prep, 1)

            def project(b, i, step):
                t = b * QT + i
                if step == 5:
                    pool.wait_ge(rope_parts, t + 1)
                    nc.gpsimd.tensor_tensor(rope_cos[:], rope_cos[:], rope_sin[:], ALU.add).then_inc(rope_done, 1)

            def close(b, i, step):
                T, r = b * QT + i, i % 2
                if step == 5:
                    pool.wait_ge(post_eps, T + 1)
                    nc.gpsimd.tensor_tensor(post_rstd[:, r:r + 1], post_var[:, r:r + 1], half[:, 0:1], ALU.pow
                                            ).then_inc(post_scale, 1)
                    pool.wait_ge(y_norm, T + 1)
                    tile = xt[:, bass.ds(T, 1), :].rearrange("p o e -> p (o e)")
                    nc.gpsimd.tensor_tensor(tile, tile, y_sb[:, r], ALU.add).then_inc(x1_ready, 1)
                if step == 7:
                    pool.wait_ge(post2_eps, T + 1)
                    nc.gpsimd.tensor_tensor(post_rstd[:, r:r + 1], post_var[:, r:r + 1], half[:, 0:1], ALU.pow
                                            ).then_inc(post2_scale, 1)

            def project_batch_norm(b):
                pool.wait_ge(ln1_eps, b + 1)
                nc.gpsimd.tensor_tensor(ln1_rstd[:], ln1_var[:], half[:], ALU.pow).then_inc(ln1_scale, 1)

            def slot(b, f, side_project, side_close, before):
                for pos in range(NC):
                    if pos == 0 and side_project is not None:
                        project_batch_norm(side_project)
                    if side_project is not None:
                        for i, s in project_steps(pos):
                            project(side_project, i, s)
                    if side_close is not None:
                        for i, s in close_steps(pos):
                            close(side_close, i, s)

            project_batch_norm(0)
            for i in range(QT):
                project(0, i, 5)
            slot(0, 0, None, None, None)
            with pool.Fori(0, BATCHES - 1) as b:
                slot(b, 1, b + 1, None, (b, 0, NPAIR - 1))
                slot(b + 1, 0, None, b, (b, 1, NPAIR - 1))
            slot(BATCHES - 1, 1, None, None, (BATCHES - 1, 0, NPAIR - 1))
            for pos in range(NC):
                for i, s in close_steps(pos):
                    close(BATCHES - 1, i, s)

            pool.wait_ge(gates_ready, TILES)

            def weights(ep, slot):
                e = 2 * ep + slot
                pool.wait_ge(w_load[slot], 32 * ep + 32)
                alone(pool)
                nc.gpsimd.tensor_copy(w13h[:, slot], w13f[:, slot]).then_inc(wh_made, 1)
                nc.gpsimd.tensor_copy(w2h[:, slot], w2f[:, slot]).then_inc(wh_made, 1)
                pool.wait_ge(wh_made, 2 * e + 2)
                nc.gpsimd.tensor_tensor(w13l[:, slot], w13f[:, slot], f32(w13h[:, slot]), ALU.subtract)
                nc.gpsimd.tensor_tensor(w2l[:, slot], w2f[:, slot], f32(w2h[:, slot]), ALU.subtract
                                        ).then_inc(w_split, 1)

            def hidden_low(ep, n):
                u = UNITS * ep + n
                pool.wait_ge(hidh_ready, u + 1)
                nc.gpsimd.tensor_tensor(hidl[:, n % 4], hid[:, n % 2], f32(hidh[:, n % 4]), ALU.subtract
                                        ).then_inc(hidl_ready, 1)

            weights(0, 0)
            weights(0, 1)
            hidden_low(0, 0)
            hidden_low(0, 1)
            with pool.Fori(0, EPAIRS - 1) as ep:
                for n in range(2, UNITS + 2):
                    hidden_low(ep + n // UNITS, n % UNITS)
                    if n == 5:
                        pool.wait_ge(down_psum, UNITS * ep + CHUNKS)
                        weights(ep + 1, 0)
                pool.wait_ge(down_psum, UNITS * ep + UNITS)
                weights(ep + 1, 1)
            for n in range(2, UNITS):
                hidden_low(EPAIRS - 1, n)

            for t in range(TILES):
                pool.wait_ge(fin_eps, t + 1)
                nc.gpsimd.tensor_tensor(fin_rstd[:, t:t + 1], fin_var[:, t:t + 1], half[:, 0:1], ALU.pow
                                        ).then_inc(fin_scale, 1)
                pool.wait_ge(fin_norm, t + 1)
                nc.gpsimd.tensor_tensor(ybuf[:, t, :], ybuf[:, t, :], xt[:, t, :], ALU.add
                                        ).then_inc(fin_ready, 1)

        @block.scalar
        def _(act):
            act.sem_inc(exp_done, 2)

            def project(b, i, step):
                t = b * QT + i
                if step == 2:
                    act.wait_ge(xnT_psum, t + 1)
                    wait(act, qkv_psum, t)
                    nc.scalar.copy(xnT[:], bank[XT][:, 0:EMB].rearrange("p (c n) -> p c n", c=KC)
                                   ).then_inc(xnT_ready, 1)
                if step == 4:
                    act.wait_ge(qkv_psum, t + 1)
                    if i == 0:
                        wait(act, v_ready, 4 * b)
                    nc.scalar.copy(v_stage[:, i], bank[VB][:, 0:EMB].rearrange("p (h d) -> p h d", h=HEADS)
                                   ).then_inc(v_staged, 1)
                if step == 7:
                    act.wait_ge(qkT_psum, t + 1)
                    wait(act, s_spill, 32 * t)
                    nc.scalar.copy(qkTh[:], bank[SCORE[i % 2]][:, :].rearrange("p (w n) -> p w n", w=4)
                                   ).then_inc(qkTh_ready, 1)

            def place_v(b, f):
                act.wait_ge(v_staged, QT * b + QT)
                if not isinstance(b, int):
                    act.wait_ge(pv_psum, 2 * (2 * b + f - 1) * NPAIR + 4)
                for h in range(2):
                    nc.scalar.copy(vs[:, f, :, :, 2 * h, 0:HD], v_stage[:, :, f * HALF + h:(f + 1) * HALF:2]
                                   ).then_inc(v_ready, 1)

            def maxima_out(b, f):
                u = 2 * b + f
                act.wait_ge(maxT_psum, u + 1)
                wait(act, s_max_out, 16 * u)
                rows = slice(f * P // 2, (f + 1) * P // 2)
                nc.scalar.copy(maxT[rows], bank[SCORE[0]][rows, 0:P]).then_inc(maxT_ready, 1)

            def close(b, i, step):
                T, r = b * QT + i, i % 2
                if step == 2:
                    act.wait_ge(attnT_psum, T + 2)
                    nc.scalar.copy(attnT[:, r], bank[QK][:, 0:EMB].rearrange("p (c n) -> p c n", c=KC)
                                   ).then_inc(attnT_ready, 1)
                if step == 9:
                    act.wait_ge(xn2T_psum, T + 1)
                    xn2T = bank[XT][:, 0:EMB].rearrange("p (c n) -> p c n", c=KC)
                    nc.scalar.copy(x2T_tile[:, r], xn2T)
                    nc.scalar.copy(x2T[:, :, bass.ds(T * P, P)], xn2T).then_inc(x2T_ready, 1)
                if step == 11:
                    act.wait_ge(router_psum, T + 1)
                    nc.scalar.copy(logits[:, r], bank[XT][:, EMB:EMB + EXPERTS]).then_inc(logits_ready, 1)
                if step == 13:
                    act.wait_ge(negtop_ready, T + 1)
                    nc.scalar.activation(expl[:, r], logits[:, r], ACTF.Exp, bias=negtop[:, r:r + 1]
                                         ).then_inc(expl_ready, 1)

            def exponentials(b, f, c):
                u = 2 * b + f
                n = u * NC + c
                act.wait_ge(weigh_psum, n + 1)
                if c % 5 == 0:
                    act.wait_ge(pv_psum, 2 * (u * NPAIR + c // 5) + 2)
                nc.scalar.activation(probs[:, c % RING], bank[WEIGH[c % 2]][:, :], ACTF.Exp).then_inc(exp_done, 1)

            def copy_transposed(b, f, p):
                n = (2 * b + f) * NPAIR + p
                act.wait_ge(pv_psum, 2 * n + 6)
                nc.scalar.copy(oT[0:2 * VW], bank[OB][0:2 * VW, :]).then_inc(oT_ready, 1)

            def slot(b, f, side_project, side_close, before):
                for pos in range(NC):
                    if side_project is None and f == 0 and pos == 4:
                        place_v(b, 1)
                    exponentials(b, f, pos)
                    if pos == 1 and before is not None:
                        copy_transposed(*before)
                    if pos > 5 and pos % 5 == 1:
                        copy_transposed(b, f, pos // 5 - 1)
                    if side_project is not None:
                        for i, s in project_steps(pos):
                            project(side_project, i, s)
                        if pos == NC - 1:
                            place_v(side_project, 0)
                    if side_close is not None:
                        for i, s in close_steps(pos):
                            close(side_close, i, s)
                    if side_project is None and f == 0 and pos == 16:
                        maxima_out(b, 1)
                    if side_project is not None and pos == 18:
                        maxima_out(side_project, 0)

            for pos in range(NC):
                for i, s in project_steps(pos):
                    project(0, i, s)
            place_v(0, 0)
            maxima_out(0, 0)
            slot(0, 0, None, None, None)
            with act.Fori(0, BATCHES - 1) as b:
                slot(b, 1, b + 1, None, (b, 0, NPAIR - 1))
                slot(b + 1, 0, None, b, (b, 1, NPAIR - 1))
            slot(BATCHES - 1, 1, None, None, (BATCHES - 1, 0, NPAIR - 1))
            copy_transposed(BATCHES - 1, 1, NPAIR - 1)
            for pos in range(NC):
                for i, s in close_steps(pos):
                    close(BATCHES - 1, i, s)

            act.wait_ge(gates_ready, TILES)
            for c in range(KC):
                nc.scalar.copy(xh[:, c], x2T[:, c]).then_inc(xh_cut, 1)

            def unit(ep, n):
                u = UNITS * ep + n
                act.wait_ge(gu_psum, u + 1)
                nc.scalar.activation(silu[:, n % 2], bank[n % 2][0:FF, :], ACTF.Silu).then_inc(silu_ready, 1)
                act.wait_ge(hid_ready, u + 1)
                nc.scalar.copy(hidh[:, n % 4], hid[:, n % 2]).then_inc(hidh_ready, 1)

            with act.Fori(0, EPAIRS) as ep:
                for n in range(UNITS):
                    unit(ep, n)

        @block.vector
        def _(dve):
            dve.sem_inc(max_done, 2)
            nc.vector.memset(half[:], -0.5).then_inc(s_prep, 1)
            dve.wait_ge(s_const, 16 * 6)
            nc.vector.tensor_copy(ident_b[:], ident_f[:]).then_inc(s_prep, 1)
            nc.vector.tensor_copy(mask_b[:], mask_f).then_inc(s_prep, 1)

            def tile_of(buf, T):
                return buf[:, bass.ds(T, 1), :].rearrange("p o e -> p (o e)")

            def mean_var(n, stat, mv, var, src, s_bn, s_mean, s_eps):
                alone(dve)
                nc.vector.bn_stats(stat, src).then_inc(s_bn, 1)
                dve.wait_ge(s_bn, n + 1)
                alone(dve)
                nc.vector.bn_aggr(mv, stat).then_inc(s_mean, 1)
                dve.wait_ge(s_mean, n + 1)
                nc.vector.tensor_scalar(var, mv[:, 1:2], EPS, None, ALU.add).then_inc(s_eps, 1)

            def batch_norm_stats(b):
                dve.wait_ge(s_x, 16 * b + 16)
                alone(dve)
                for i in range(QT):
                    nc.vector.bn_stats(ln1_stat[:, i], tile_of(xt, b * QT + i)).then_inc(ln1_bn, 1)
                dve.wait_ge(ln1_bn, QT * b + QT)
                alone(dve)
                for i in range(QT):
                    nc.vector.bn_aggr(ln1_mv[:, i], ln1_stat[:, i]).then_inc(ln1_mean, 1)
                dve.wait_ge(ln1_mean, QT * b + QT)
                nc.vector.tensor_scalar(ln1_var[:], ln1_mv[:, :, 1], EPS, None, ALU.add).then_inc(ln1_eps, 1)

            def project(b, i, step):
                t = b * QT + i
                if step == 0:
                    if i == 0:
                        dve.wait_ge(ln1_scale, b + 1)
                    wait(dve, xnT_psum, t)
                    nc.vector.tensor_scalar(xn[:], tile_of(xt, t), ln1_mv[:, i, 0:1], ln1_rstd[:, i:i + 1],
                                            ALU.subtract, ALU.mult).then_inc(xn_ready, 1)
                if step == 4:
                    dve.wait_ge(qkv_psum, t + 1)
                    wait(dve, qkT_psum, t)
                    qk = bank[QK][:, :].rearrange("p (w h d) -> p w h d", w=2, h=HEADS)
                    cos = rope_sb[:, i, 0].unsqueeze(2)
                    sin = rope_sb[:, i, 1].unsqueeze(2)
                    nc.vector.tensor_tensor(rope_cos[:], qk, cos.broadcast_to([P, 2, HEADS, HD]), ALU.mult)
                    for o in range(2):
                        last = nc.vector.tensor_tensor(rope_sin[:, :, :, o::2], qk[:, :, :, 1 - o::2],
                                                       sin[:, :, :, o::2].broadcast_to([P, 2, HEADS, HD // 2]), ALU.mult)
                    last.then_inc(rope_parts, 1)
                if step == 7:
                    dve.wait_ge(qkTh_ready, t + 1)
                    wait(dve, s_spill, 32 * t)
                    nc.vector.tensor_tensor(qkTl[:], bank[SCORE[i % 2]][:, :].rearrange("p (w n) -> p w n", w=4),
                                            f32(qkTh[:]), ALU.subtract).then_inc(qkTl_ready, 1)

            def row_maxima(b, f, c):
                u = 2 * b + f
                dve.wait_ge(score_psum, u * NC + c + 1)
                if c == 0:
                    wait(dve, maxl_ready, u)
                places = PAIR_BANKS[c % 5]
                h0 = 2 * (c // 5)
                S = bank[SCORE[c % 2]]
                if len(places) == 2 and places[0][1] == places[1][1]:
                    i = places[0][1]
                    last = nc.vector.tensor_reduce(negmax[:, i, h0:h0 + 2], S[:, :].rearrange("p (a l) -> p a l", a=2),
                                                   AXX, ALU.max, negate=True)
                else:
                    for h, i, col in places:
                        last = nc.vector.tensor_reduce(negmax[:, i, h0 + h:h0 + h + 1], S[:, col:col + P * (i + 1)],
                                                       AXX, ALU.max, negate=True)
                last.then_inc(max_done, 1)

            def cut_maxima(b, f):
                u = 2 * b + f
                dve.wait_ge(max_done, u * NC + NC + 2)
                wait(dve, maxT_psum, u)
                nc.vector.tensor_copy(maxhl[:, f, :, 0, :].bitcast(F32R), negmax[:]).then_inc(maxh_ready, 1)
                dve.wait_ge(maxh_ready, u + 1)
                nc.vector.tensor_tensor(maxhl[:, f, :, 1, :], negmax[:], maxhl[:, f, :, 0, :], ALU.subtract
                                        ).then_inc(maxl_ready, 1)

            def normalise(b, f, p):
                n = (2 * b + f) * NPAIR + p
                dve.wait_ge(o_psum, n + 1)
                O = bank[OB][:, :].rearrange("p (i n) -> p i n", i=QT)[:, :, 0:2 * VW].rearrange("p i (a v) -> p a i v", a=2)
                wait(dve, attn_ready, n)
                nc.vector.reciprocal(o_inv[:], O[:, :, :, HD]).then_inc(inv_ready, 1)
                goal = attn[:, :, HALF + 2 * p:HALF + 2 * p + 2] if f == 1 else attn_first[:, :, 2 * p:2 * p + 2]
                dve.wait_ge(inv_ready, n + 1)
                nc.vector.tensor_tensor(goal.rearrange("p i a d -> p a i d"), O[:, :, :, 0:HD],
                                        o_inv[:].unsqueeze(3).broadcast_to([P, 2, QT, HD]), ALU.mult
                                        ).then_inc(attn_ready, 1)

            def join_halves(b):
                dve.wait_ge(attn_ready, (2 * b + 1) * NPAIR)
                dve.wait_ge(attnT_psum, QT * b + 1)
                nc.vector.tensor_copy(attn[:, :, 0:HALF], attn_first[:]).then_inc(joined, 1)

            def close(b, i, step):
                T, r = b * QT + i, i % 2
                if step == 4:
                    dve.wait_ge(wo_psum, T + 1)
                    mean_var(T, post_stat[:, r], post_mv[:, r], post_var[:, r:r + 1], bank[VB][:, 0:EMB],
                             post_bn, post_mean, post_eps)
                if step == 5:
                    dve.wait_ge(post_scale, T + 1)
                    nc.vector.tensor_scalar(y_sb[:, r], bank[VB][:, 0:EMB], post_mv[:, r, 0:1], post_rstd[:, r:r + 1],
                                            ALU.subtract, ALU.mult).then_inc(y_norm, 1)
                if step == 6:
                    dve.wait_ge(x1_ready, T + 1)
                    mean_var(T, post_stat[:, r], post_mv[:, r], post_var[:, r:r + 1], tile_of(xt, T),
                             post2_bn, post2_mean, post2_eps)
                if step == 7:
                    dve.wait_ge(post2_scale, T + 1)
                    nc.vector.tensor_scalar(xn2[:, r], tile_of(xt, T), post_mv[:, r, 0:1], post_rstd[:, r:r + 1],
                                            ALU.subtract, ALU.mult).then_inc(xn2_ready, 1)
                if step == 12:
                    dve.wait_ge(logits_ready, T + 1)
                    alone(dve)
                    nc.vector.max(top[:, r], logits[:, r]).then_inc(top_ready, 1)
                    dve.wait_ge(top_ready, T + 1)
                    nc.vector.tensor_scalar(negtop[:, r:r + 1], top[:, r, 0:1], -1.0, None, ALU.mult
                                            ).then_inc(negtop_ready, 1)
                    nc.vector.match_replace(struck[:, r], top[:, r], logits[:, r], -3.0e38).then_inc(struck_ready, 1)
                    dve.wait_ge(struck_ready, T + 1)
                    nc.vector.tensor_tensor(chosen[:, r], struck[:, r], logits[:, r], ALU.not_equal
                                            ).then_inc(chosen_ready, 1)
                if step == 13:
                    dve.wait_ge(expl_ready, T + 1)
                    dve.wait_ge(chosen_ready, T + 1)
                    nc.vector.tensor_tensor(picked[:, r], expl[:, r], chosen[:, r], ALU.mult).then_inc(picked_ready, 1)
                    dve.wait_ge(picked_ready, T + 1)
                    nc.vector.reduce_sum(gsum[:, r:r + 1], picked[:, r], AXX).then_inc(gsum_ready, 1)
                    dve.wait_ge(gsum_ready, T + 1)
                    nc.vector.reciprocal(ginv[:, r:r + 1], gsum[:, r:r + 1]).then_inc(ginv_ready, 1)
                    dve.wait_ge(ginv_ready, T + 1)
                    nc.vector.tensor_scalar(tile_of(gates, T), picked[:, r], ginv[:, r:r + 1], None, ALU.mult
                                            ).then_inc(gates_ready, 1)

            def slot(b, f, side_project, side_close, before):
                for pos in range(NC):
                    if pos == 0 and side_project is not None:
                        batch_norm_stats(side_project)
                    if pos == 3 and before is not None:
                        normalise(*before)
                        if f == 1:
                            join_halves(b)
                    if pos > 5 and pos % 5 == 3:
                        normalise(b, f, pos // 5 - 1)
                    if side_project is not None:
                        for i, s in project_steps(pos):
                            project(side_project, i, s)
                        for c in late_scores(pos):
                            row_maxima(side_project, 0, c)
                        if pos == 17:
                            cut_maxima(side_project, 0)
                    elif f == 0:
                        for c in early_scores(pos):
                            row_maxima(b, 1, c)
                        if pos == 15:
                            cut_maxima(b, 1)
                    if side_close is not None:
                        for i, s in close_steps(pos):
                            close(side_close, i, s)

            batch_norm_stats(0)
            for pos in range(NC):
                for i, s in project_steps(pos):
                    project(0, i, s)
            for c in range(NC):
                row_maxima(0, 0, c)
            cut_maxima(0, 0)
            slot(0, 0, None, None, None)
            with dve.Fori(0, BATCHES - 1) as b:
                slot(b, 1, b + 1, None, (b, 0, NPAIR - 1))
                slot(b + 1, 0, None, b, (b, 1, NPAIR - 1))
            slot(BATCHES - 1, 1, None, None, (BATCHES - 1, 0, NPAIR - 1))
            normalise(BATCHES - 1, 1, NPAIR - 1)
            for pos in range(NC):
                for i, s in close_steps(pos):
                    close(BATCHES - 1, i, s)

            dve.wait_ge(gates_ready, TILES)
            for c in range(KC):
                dve.wait_ge(xh_cut, c + 1)
                nc.vector.tensor_tensor(xl[:, c], x2T[:, c], f32(xh[:, c]), ALU.subtract).then_inc(xl_cut, 1)
            for c in range(2):
                nc.vector.memset(acc[:, c * TILES // 2:(c + 1) * TILES // 2], 0.0).then_inc(acc_done, 1)

            def hidden(ep, n, first=False):
                u = UNITS * ep + n
                dve.wait_ge(silu_ready, u + 1)
                if not first:
                    dve.wait_ge(hidl_ready, u - 1)
                nc.vector.tensor_tensor(hid[:, n % 2], silu[:, n % 2], bank[2 + n % 2][0:FF, :], ALU.mult
                                        ).then_inc(hid_ready, 1)

            def gather_up(ep, n):
                u = UNITS * ep + n
                e = 2 * ep + n // CHUNKS
                c = n % CHUNKS
                dve.wait_ge(down_psum, u + 1)
                dve.wait_ge(acc_done, u + 2)
                for k in range(4):
                    t = 4 * c + k
                    r = nc.vector.scalar_tensor_tensor(
                        acc[:, t, :], bank[4 + 2 * (n % 2) + k // 2][:, (k % 2) * EMB:(k % 2 + 1) * EMB],
                        gates[:, t, bass.ds(e, 1)], acc[:, t, :], ALU.mult, ALU.add)
                r.then_inc(acc_done, 1)

            hidden(0, 0, first=True)
            hidden(0, 1, first=True)
            with dve.Fori(0, EPAIRS - 1) as ep:
                for n in range(2, UNITS + 2):
                    hidden(ep + n // UNITS, n % UNITS)
                    gather_up(ep, n - 2)
            ep = EPAIRS - 1
            for n in range(2, UNITS + 2):
                if n < UNITS:
                    hidden(ep, n)
                gather_up(ep, n - 2)

            for t in range(TILES):
                dve.wait_ge(acc_done, UNITS * EPAIRS + 2)
                mean_var(t, fin_stat[:, t], fin_mv[:, t], fin_var[:, t:t + 1], acc[:, t, :], fin_bn, fin_mean, fin_eps)
            for t in range(TILES):
                dve.wait_ge(fin_scale, t + 1)
                nc.vector.tensor_scalar(ybuf[:, t, :], acc[:, t, :], fin_mv[:, t, 0:1], fin_rstd[:, t:t + 1],
                                        ALU.subtract, ALU.mult).then_inc(fin_norm, 1)

        @block.tensor
        def _(pe):
            pe.sem_inc(pv_psum, 4)
            pe.sem_inc(attnT_psum, 1)
            pe.wait_ge(s_const, 16 * 6)
            pe.wait_ge(s_prep, 3)
            pe.wait_ge(s_ones, 7)

            def transpose2(dst, src):
                for c in range(KC):
                    last = nc.tensor.matmul(dst[:, c * P:(c + 1) * P], src[:, c * P:(c + 1) * P], ident_f[:],
                                            is_transpose=True, start=True, stop=True)
                return last

            def product(dst, a, w):
                for c in range(KC):
                    last = nc.tensor.matmul(dst, a[:, c], w[:, c], start=(c == 0), stop=(c == KC - 1))
                return last

            def project(b, i, step):
                t = b * QT + i
                if step == 1:
                    pe.wait_ge(xn_ready, t + 1)
                    wait(pe, xnT_ready, t)
                    transpose2(bank[XT], xn).then_inc(xnT_psum, 1)
                if step == 3:
                    pe.wait_ge(xnT_ready, t + 1)
                    wait(pe, rope_parts, t)
                    wait(pe, v_staged, t)
                    product(bank[QK][:, :], xnT, wqkv_sb[:, :, 0:2 * EMB])
                    product(bank[VB][:, 0:EMB], xnT, wqkv_sb[:, :, 2 * EMB:]).then_inc(qkv_psum, 1)
                if step == 6:
                    pe.wait_ge(rope_done, t + 1)
                    wait(pe, qkTl_ready, t)
                    for w in range(4):
                        last = nc.tensor.matmul(
                            bank[SCORE[i % 2]][:, w * P:(w + 1) * P],
                            rope_cos[:, w // 2, (w % 2) * HALF:(w % 2 + 1) * HALF].rearrange("p h d -> p (h d)"),
                            ident_f[:], is_transpose=True, start=True, stop=True)
                    last.then_inc(qkT_psum, 1)

            def add_masks(S, cols, a, w):
                first, last = cols[0] // P, cols[-1] // P
                blocks = S[:, :].rearrange("p (a n) -> p a n", n=P)[:, first:last + 1:max(last - first, 1)]
                nc.tensor.matmul(blocks, a[:], w[:].unsqueeze(1).broadcast_to([P, len(cols), P]),
                                 start=True, stop=False, skip_group_check=True)

            def scores(b, f, c):
                u = 2 * b + f
                if c == 0:
                    pe.wait_ge(s_load, LOADS * u + LOADS)
                    wait(pe, maxT_ready, u)
                pe.wait_ge(max_done, u * NC + c + 1)
                S = bank[SCORE[c % 2]]
                add_masks(S, [col + P * i for h, i, col in PAIR_BANKS[c % 5]], ident_b, mask_b)
                for h, i, col in PAIR_BANKS[c % 5]:
                    a = 2 * (c // 5) + h
                    L = P * (i + 1)
                    last = nc.tensor.matmul(S[:, col:col + L], qs[f][:, a, i * P:(i + 1) * P], ks[f][:, a, 0:L],
                                            start=False, stop=True, skip_group_check=True)
                last.then_inc(score_psum, 1)

            def transpose_maxima(b, f):
                u = 2 * b + f
                pe.wait_ge(maxl_ready, u + 1)
                wait(pe, maxT_ready, u)
                nc.tensor.matmul(bank[SCORE[0]][:, 0:P],
                                 maxhl[:].rearrange("p f i c a -> p (f i c a)"), ident_f[:],
                                 is_transpose=True, start=True, stop=True).then_inc(maxT_psum, 1)

            def weigh(b, f, c):
                u = 2 * b + f
                if c == 0:
                    pe.wait_ge(s_max_in, 16 * u + 16)
                pe.wait_ge(exp_done, u * NC + c + 1)
                S = bank[WEIGH[c % 2]]
                add_masks(S, [col for h, r, col in PAIR_BANKS[c % 5]], mask_b, ident_b)
                for h, r, col in PAIR_BANKS[c % 5]:
                    a = 2 * (c // 5) + h
                    j, N = QT - 1 - r, P * (r + 1)
                    last = nc.tensor.matmul(S[:, col:col + N], ks[f][:, a, j * P:(j + 1) * P], qs[f][:, a, j * P:],
                                            start=False, stop=True, skip_group_check=True)
                last.then_inc(weigh_psum, 1)

            def weigh_values(b, f, p, h):
                u = 2 * b + f
                n = u * NPAIR + p
                if h == 0:
                    if p == 0:
                        pe.wait_ge(v_ready, 2 * u + 2)
                    wait(pe, attn_ready, n)
                pe.wait_ge(exp_done, u * NC + 5 * p + 3 + 2 * h + 2)
                for j in range(QT):
                    w, col = KPLACE[(h, j)]
                    last = nc.tensor.matmul(
                        bank[OB][0:2 * VW, j * P:], vs[:, f, j, p, h:h + 2].rearrange("p a v -> p (a v)"),
                        probs[:, (5 * p + w) % RING, col:col + (QT - j) * P], start=(h == 0 and j == 0),
                        stop=(h == 1 and j == QT - 1), skip_group_check=True)
                last.then_inc(pv_psum, 1)

            def transpose_output(b, f, p):
                n = (2 * b + f) * NPAIR + p
                pe.wait_ge(oT_ready, n + 1)
                for i in range(QT):
                    last = nc.tensor.matmul(bank[OB][:, i * P:(i + 1) * P], oT[:, i * P:(i + 1) * P], ident_f[:],
                                            is_transpose=True, start=True, stop=True)
                last.then_inc(o_psum, 1)

            def close(b, i, step):
                T, r = b * QT + i, i % 2
                if step == 1:
                    pe.wait_ge(attn_ready, 2 * NPAIR * (b + 1))
                    pe.wait_ge(joined, b + 1)
                    if i > 0:
                        pe.wait_ge(attnT_ready, T)
                    transpose2(bank[QK], attn[:, i].rearrange("p h d -> p (h d)")).then_inc(attnT_psum, 1)
                if step == 3:
                    pe.wait_ge(attnT_ready, T + 1)
                    if i > 0:
                        pe.wait_ge(y_norm, T)
                    product(bank[VB][:, 0:EMB], attnT[:, r], wo_sb).then_inc(wo_psum, 1)
                if step == 8:
                    pe.wait_ge(xn2_ready, T + 1)
                    if i > 0:
                        pe.wait_ge(logits_ready, T)
                    transpose2(bank[XT][:, 0:EMB], xn2[:, r]).then_inc(xn2T_psum, 1)
                if step == 10:
                    pe.wait_ge(x2T_ready, T + 1)
                    product(bank[XT][:, EMB:EMB + EXPERTS], x2T_tile[:, r], wg_sb).then_inc(router_psum, 1)

            def slot(b, f, side_project, side_close, before):
                weigh(b, f, 0)
                for pos in range(NC):
                    if pos + 1 < NC:
                        weigh(b, f, pos + 1)
                    if pos == 0 and before is not None:
                        weigh_values(*before, 1)
                    if pos == 2 and before is not None:
                        transpose_output(*before)
                    if pos % 5 == 4:
                        weigh_values(b, f, pos // 5, 0)
                    if pos >= 5 and pos % 5 == 0:
                        weigh_values(b, f, pos // 5 - 1, 1)
                    if pos >= 5 and pos % 5 == 2:
                        transpose_output(b, f, pos // 5 - 1)
                    if side_project is not None:
                        for i, s in project_steps(pos):
                            project(side_project, i, s)
                        for c in late_scores(pos):
                            scores(side_project, 0, c)
                        if pos == 18:
                            transpose_maxima(side_project, 0)
                    elif f == 0:
                        for c in early_scores(pos):
                            scores(b, 1, c)
                        if pos == 16:
                            transpose_maxima(b, 1)
                    if side_close is not None:
                        for i, s in close_steps(pos):
                            close(side_close, i, s)

            for pos in range(NC):
                for i, s in project_steps(pos):
                    project(0, i, s)
            for c in range(NC):
                scores(0, 0, c)
            transpose_maxima(0, 0)
            slot(0, 0, None, None, None)
            with pe.Fori(0, BATCHES - 1) as b:
                slot(b, 1, b + 1, None, (b, 0, NPAIR - 1))
                slot(b + 1, 0, None, b, (b, 1, NPAIR - 1))
            slot(BATCHES - 1, 1, None, None, (BATCHES - 1, 0, NPAIR - 1))
            weigh_values(BATCHES - 1, 1, NPAIR - 1, 1)
            transpose_output(BATCHES - 1, 1, NPAIR - 1)
            for pos in range(NC):
                for i, s in close_steps(pos):
                    close(BATCHES - 1, i, s)

            def gate_up(ep, n, first=False):
                u = UNITS * ep + n
                slot, c = n // CHUNKS, n % CHUNKS
                if c == 0:
                    pe.wait_ge(w_split, 2 * ep + slot + 1)
                if not first:
                    pe.wait_ge(hid_ready, u - 1)
                for dst, f0 in ((bank[n % 2], 0), (bank[2 + n % 2], FF)):
                    k = 0
                    for kc in range(KC):
                        for w, xx in ((w13h, xh), (w13h, xl), (w13l, xh)):
                            r = nc.tensor.matmul(dst[0:FF, :], w[:, slot, kc, f0:f0 + FF],
                                                 xx[:, kc, c * 512:(c + 1) * 512], start=(k == 0), stop=(k == 5))
                            k += 1
                r.then_inc(gu_psum, 1)

            def down(ep, n):
                u = UNITS * ep + n
                slot = n // CHUNKS
                pe.wait_ge(hidh_ready, u + 1)
                pe.wait_ge(hidl_ready, u + 1)
                pe.wait_ge(acc_done, u + 1)
                for k in range(4):
                    dst = bank[4 + 2 * (n % 2) + k // 2][:, (k % 2) * EMB:(k % 2 + 1) * EMB]
                    for m, (hh, w) in enumerate(((hidh, w2h), (hidh, w2l), (hidl, w2h))):
                        r = nc.tensor.matmul(dst, hh[:, n % 4, k * P:(k + 1) * P], w[:, slot, :],
                                             start=(m == 0), stop=(m == 2))
                r.then_inc(down_psum, 1)

            pe.wait_ge(gates_ready, TILES)
            pe.wait_ge(xl_cut, KC)
            gate_up(0, 0, first=True)
            gate_up(0, 1, first=True)
            with pe.Fori(0, EPAIRS - 1) as ep:
                for n in range(2, UNITS + 2):
                    gate_up(ep + n // UNITS, n % UNITS)
                    down(ep, n - 2)
            ep = EPAIRS - 1
            for n in range(2, UNITS + 2):
                if n < UNITS:
                    gate_up(ep, n)
                down(ep, n - 2)


_INS = ['L0_attn_x', 'L0_attn_Wqkv', 'L0_attn_Wo', 'L0_ffn_wg', 'L0_ffn_w1', 'L0_ffn_v1', 'L0_ffn_w2']


def kernel(**inputs):
    import numpy as np
    import concourse.bacc as bacc
    from concourse import mybir as mb
    from concourse.bass_utils import run_bass_kernel_spmd

    x, wqkv, wo, wg, w1, v1, w2 = (np.ascontiguousarray(inputs[n]) for n in _INS)
    f = np.float32
    inv = (f(1.0) / np.power(f(10000.0), f(2.0) * np.arange(HD // 2, dtype=f) / f(HD))).astype(f)
    angle = np.outer(np.arange(SEQ, dtype=f), inv).astype(f)
    cos, sin = np.cos(angle).astype(f), np.sin(angle).astype(f)
    table = np.stack([np.repeat(cos, 2, axis=1), np.stack([-sin, sin], axis=2).reshape(SEQ, HD)], axis=1)
    rope = np.ascontiguousarray(np.stack([table * f(0.25), table], axis=2))
    arrays = {
        "x": x, "wqkv": wqkv, "wo": wo,
        "wgT": np.ascontiguousarray(wg.T),
        "w13": np.ascontiguousarray(np.concatenate([w1, v1], axis=2)),
        "w2": w2,
        "ident": np.eye(P, dtype=f),
        "mask": np.triu(np.full((P, P), -1e30, dtype=f), 1),
        "rope": rope,
    }
    nc = bacc.Bacc("TRN2", target_bir_lowering=False, num_devices=1)
    args = [nc.dram_tensor(n, a.shape, mb.dt.from_np(a.dtype), kind="ExternalInput").ap() for n, a in arrays.items()]
    args.append(nc.dram_tensor("out", (BATCHES, SEQ, EMB), mb.dt.float32, kind="ExternalOutput").ap())
    build(nc, *args)
    r = run_bass_kernel_spmd(nc, [arrays], core_ids=[0])
    return r.results[0]["out"]
```

```python
import concourse.bass as bass
from concourse import mybir
from contextlib import ExitStack

F32 = mybir.dt.float32
F32R = mybir.dt.float32r
BF16 = mybir.dt.bfloat16
ACTF = mybir.ActivationFunctionType
ALU = mybir.AluOpType
AXX = mybir.AxisListType.X

P = 128
BATCHES, SEQ, EMB = 4, 512, 256
TOKENS = BATCHES * SEQ
TILES = TOKENS // P
QT = SEQ // P
KC = EMB // P
HEADS, HD = 16, 16
HALF = HEADS // 2
LOADS = 16 * 9
ROWS = 4 * HD + 2
VW = HD + 1
EXPERTS, TOPK, FF = 32, 8, 96
CHUNKS = TOKENS // 512
EPS = 1e-5

HIGH = P - FF

PAIR_BANKS = [[(0, 3, 0)], [(0, 2, 0), (0, 0, 384)], [(0, 1, 0), (1, 1, 256)], [(1, 3, 0)], [(1, 2, 0), (1, 0, 384)]]
NPAIR = HALF // 2
NC = len(PAIR_BANKS) * NPAIR
KPLACE = {(h, 3 - r): (w, col) for w, bank in enumerate(PAIR_BANKS) for h, r, col in bank}
RING = 2 * len(PAIR_BANKS)
CLOSE_AT = {1: 0, 2: 0, 3: 1, 4: 1, 5: 2, 6: 3, 7: 4, 8: 5, 9: 5, 10: 6, 11: 7, 12: 7, 13: 8}
PROJECT_AT = {0: 0, 1: 0, 2: 1, 3: 1, 4: 2, 5: 3, 6: 3, 7: 4}


def close_steps(pos):
    return [(i, s) for i in range(QT) for s, at in CLOSE_AT.items() if 4 + 2 * i + at == pos]


def project_steps(pos):
    return [(i, s) for i in range(QT) for s, at in PROJECT_AT.items() if 3 * i // 2 + at == pos]


def early_scores(pos):
    return [c for c in range(NC) if 4 + c * 12 // NC == pos]


def late_scores(pos):
    return [c for c in range(NC) if 15 + c * 3 // NC == pos]


def wait(engine, sem, value):
    if not isinstance(value, int) or value > 0:
        engine.wait_ge(sem, value)


def build(nc, x, wqkv, wo, wgT, w13, w2, ident, mask, rope, out):
    ctx = ExitStack()
    with ctx:
        def sb(name, shape, dt=F32):
            return ctx.enter_context(nc.sbuf_tensor(name, shape, dt))

        def sem(name):
            return ctx.enter_context(nc.semaphore(name))

        def f32(ap):
            return ap.bitcast(F32)

        qk_dram = nc.dram_tensor("qk_dram", (2, P, 4, SEQ), F32).ap()
        max_dram = nc.dram_tensor("max_dram", (2, QT, 2, HALF, P), F32).ap()

        xt = sb("xt", [P, TILES, EMB])
        x2T = sb("x2T", [P, KC, TOKENS])
        gates = sb("gates", [P, TILES, EXPERTS])
        w13f = sb("w13f", [P, 2, KC, 3 * P])
        w2f = sb("w2f", [P, 2, 2, EMB])
        w13h = sb("w13h", [P, 2, KC, 3 * P], F32R)
        w13l = sb("w13l", [P, 2, KC, 3 * P], F32R)
        w2h = sb("w2h", [P, 2, 2, EMB], F32R)
        w2l = sb("w2l", [P, 2, 2, EMB], F32R)
        half = sb("half", [P, QT])

        ph1 = ExitStack()
        ph1.__enter__()

        def sb1(name, shape, dt=F32):
            return ph1.enter_context(nc.sbuf_tensor(name, shape, dt))

        ident_f = sb1("ident_f", [P, P])
        ident_b = sb1("ident_b", [P, P], BF16)
        mask_b = sb1("mask_b", [P, P], BF16)
        wqkv_sb = sb1("wqkv_sb", [P, KC, 3 * EMB])
        wo_sb = sb1("wo_sb", [P, KC, EMB])
        wg_sb = sb1("wg_sb", [P, KC, EXPERTS])
        rope_sb = sb1("rope_sb", [P, QT, 2, 2, HD])
        ln1_stat = sb1("ln1_stat", [P, QT, 6])
        ln1_mv = sb1("ln1_mv", [P, QT, 2])
        ln1_var = sb1("ln1_var", [P, QT])
        ln1_rstd = sb1("ln1_rstd", [P, QT])
        xn = sb1("xn", [P, EMB])
        xnT = sb1("xnT", [P, KC, P])
        rope_cos = sb1("rope_cos", [P, 2, HEADS, HD])
        rope_sin = sb1("rope_sin", [P, 2, HEADS, HD])
        qkTh = sb1("qkTh", [P, 4, P], F32R)
        qkTl = sb1("qkTl", [P, 4, P], F32R)
        v_stage = sb1("v_stage", [P, QT, HEADS, HD])
        vs = sb1("vs", [P, 2, QT, NPAIR, 3, VW])
        qs = [sb1(f"qs{f}", [ROWS, HALF, SEQ], F32R) for f in range(2)]
        ks = [sb1(f"ks{f}", [ROWS, HALF, SEQ], F32R) for f in range(2)]
        probs = sb1("probs", [P, RING, 512])
        mask_f = v_stage[:, 1].rearrange("p h d -> p (h d)")[:, 0:P]
        negmax = sb1("negmax", [P, QT, HALF])
        maxhl = sb1("maxhl", [P, 2, QT, 2, HALF])
        maxT = sb1("maxT", [P, P])
        oT = sb1("oT", [P, SEQ])
        zeros = oT[P - 2:P]
        o_inv = sb1("o_inv", [P, 2, QT])
        attn_first = sb1("attn_first", [P, QT, HALF, HD])
        attn = sb1("attn", [P, QT, HEADS, HD])
        attnT = sb1("attnT", [P, 2, KC, P])
        y_sb = sb1("y_sb", [P, 2, EMB])
        xn2 = y_sb
        post_stat = sb1("post_stat", [P, 2, 6])
        post_mv = sb1("post_mv", [P, 2, 2])
        post_var = sb1("post_var", [P, 2])
        post_rstd = sb1("post_rstd", [P, 2])
        x2T_tile = sb1("x2T_tile", [P, 2, KC, P])
        logits = sb1("logits", [P, 2, EXPERTS])
        top = sb1("top", [P, 2, TOPK])
        negtop = sb1("negtop", [P, 2])
        struck = sb1("struck", [P, 2, EXPERTS])
        chosen = sb1("chosen", [P, 2, EXPERTS])
        expl = sb1("expl", [P, 2, EXPERTS])
        picked = sb1("picked", [P, 2, EXPERTS])
        gsum = sb1("gsum", [P, 2])
        ginv = sb1("ginv", [P, 2])
        ph1.close()

        xh = sb("xh", [P, KC, TOKENS], F32R)
        xl = sb("xl", [P, KC, TOKENS], F32R)
        acc = sb("acc", [P, TILES, EMB])
        silu = sb("silu", [P, 2, 2, 512])
        hid = sb("hid", [P, 4, 2, 512])
        hidh = sb("hidh", [P, 4, 2, 512], F32R)
        hidl = sb("hidl", [P, 4, 2, 512], F32R)
        fin_stat = sb("fin_stat", [P, TILES, 6])
        fin_mv = sb("fin_mv", [P, TILES, 2])
        fin_var = sb("fin_var", [P, TILES])
        fin_rstd = sb("fin_rstd", [P, TILES])
        ybuf = sb("ybuf", [P, TILES, EMB])

        bank = [ctx.enter_context(nc.psum_tensor(f"bank{n}", [P, 512], F32)) for n in range(8)]
        SCORE, WEIGH, OB, QK, XT, VB = (0, 1), (2, 3), 4, 5, 6, 7

        s_const = sem("s_const")
        s_x = sem("s_x")
        s_prep = sem("s_prep")
        s_ones = sem("s_ones")
        ln1_bn = sem("ln1_bn"); ln1_mean = sem("ln1_mean"); ln1_eps = sem("ln1_eps")
        ln1_scale = sem("ln1_scale")
        xn_ready = sem("xn_ready")
        xnT_psum = sem("xnT_psum")
        xnT_ready = sem("xnT_ready")
        qkv_psum = sem("qkv_psum")
        v_staged = sem("v_staged")
        rope_parts = sem("rope_parts")
        rope_done = sem("rope_done")
        qkT_psum = sem("qkT_psum")
        qkTh_ready = sem("qkTh_ready")
        qkTl_ready = sem("qkTl_ready")
        s_spill = sem("s_spill")
        s_load = sem("s_load")
        v_ready = sem("v_ready")
        score_psum = sem("score_psum")
        max_done = sem("max_done")
        maxh_ready = sem("maxh_ready"); maxl_ready = sem("maxl_ready")
        maxT_psum = sem("maxT_psum")
        maxT_ready = sem("maxT_ready")
        s_max_out = sem("s_max_out")
        s_max_in = sem("s_max_in")
        weigh_psum = sem("weigh_psum")
        exp_done = sem("exp_done")
        pv_psum = sem("pv_psum")
        oT_ready = sem("oT_ready")
        o_psum = sem("o_psum")
        inv_ready = sem("inv_ready")
        attn_ready = sem("attn_ready")
        joined = sem("joined")
        attnT_psum = sem("attnT_psum")
        attnT_ready = sem("attnT_ready")
        wo_psum = sem("wo_psum")
        post_bn = sem("post_bn"); post_mean = sem("post_mean"); post_eps = sem("post_eps")
        post2_bn = sem("post2_bn"); post2_mean = sem("post2_mean"); post2_eps = sem("post2_eps")
        post_scale = sem("post_scale"); post2_scale = sem("post2_scale")
        y_norm = sem("y_norm")
        x1_ready = sem("x1_ready")
        xn2_ready = sem("xn2_ready")
        xn2T_psum = sem("xn2T_psum")
        x2T_ready = sem("x2T_ready")
        router_psum = sem("router_psum")
        logits_ready = sem("logits_ready")
        top_ready = sem("top_ready"); negtop_ready = sem("negtop_ready")
        struck_ready = sem("struck_ready"); chosen_ready = sem("chosen_ready")
        expl_ready = sem("expl_ready")
        picked_ready = sem("picked_ready"); gsum_ready = sem("gsum_ready")
        ginv_ready = sem("ginv_ready"); gates_ready = sem("gates_ready")
        xh_cut = sem("xh_cut")
        xl_cut = sem("xl_cut")
        w_load = [sem("w_load0"), sem("w_load1")]
        w_split = sem("w_split")
        wh_made = sem("wh_made")
        gu_psum = sem("gu_psum")
        silu_ready = sem("silu_ready")
        hid_ready = sem("hid_ready")
        hidh_ready = sem("hidh_ready")
        hidl_ready = sem("hidl_ready")
        down_psum = sem("down_psum")
        acc_done = sem("acc_done")
        fin_bn = sem("fin_bn"); fin_mean = sem("fin_mean"); fin_eps = sem("fin_eps")
        fin_scale = sem("fin_scale"); fin_norm = sem("fin_norm"); fin_ready = sem("fin_ready")
        s_out = sem("s_out")
        s_spare = sem("s_spare")

        block = ctx.enter_context(nc.Block())
        UNITS = 2 * CHUNKS
        EFOURS = EXPERTS // 4

        def alone(engine):
            engine.sem_inc(s_spare, 1)

        @block.sync
        def _(sp):
            sp.dma_start(xt[:, 0:QT, :], x[0].rearrange("(t p) e -> p t e", p=P)).then_inc(s_x, 16)
            sp.dma_start(wqkv_sb[:], wqkv.rearrange("(c p) n -> p c n", p=P)).then_inc(s_const, 16)
            sp.dma_start(ident_f[:], ident).then_inc(s_const, 16)
            sp.dma_start(rope_sb[:], rope.rearrange("(t p) a b d -> p t a b d", p=P)).then_inc(s_const, 16)
            sp.dma_start(mask_f, mask).then_inc(s_const, 16)
            sp.dma_start(wo_sb[:], wo.rearrange("(c p) n -> p c n", p=P)).then_inc(s_const, 16)
            sp.dma_start(wg_sb[:], wgT.rearrange("(c p) n -> p c n", p=P)).then_inc(s_const, 16)
            for b in range(1, BATCHES):
                sp.wait_ge(s_x, 16 * b)
                sp.dma_start(xt[:, b * QT:(b + 1) * QT, :],
                             x[b].rearrange("(t p) e -> p t e", p=P)).then_inc(s_x, 16)
            sp.wait_ge(s_ones, 8)

            def spill(b):
                for i in range(QT):
                    t = QT * b + i
                    for c, part, ready in ((0, qkTh, qkTh_ready), (1, qkTl, qkTl_ready)):
                        sp.wait_ge(ready, t + 1)
                        alone(sp)
                        sp.dma_start(qk_dram[c, :, :, i * P:(i + 1) * P], f32(part[:])).then_inc(s_spill, 16)
                    sp.wait_ge(s_spill, 32 * t + 32)
                    alone(sp)

            def load_stacks(b, f):
                u = 2 * b + f
                wait(sp, weigh_psum, (u - 2) * NC + NC)
                alone(sp)
                sp.dma_start(f32(qs[f][4 * HD:ROWS]), zeros.unsqueeze(1).broadcast_to([2, HALF, SEQ])
                             ).then_inc(s_load, 16)
                for stack, w, cuts in ((qs[f], f, (0, 1, 0, 1)), (ks[f], 2 + f, (0, 0, 1, 1))):
                    for r, c in enumerate(cuts):
                        sp.dma_start(f32(stack[r * HD:(r + 1) * HD]),
                                     qk_dram[c, :, w, :].rearrange("(a d) t -> d a t", d=HD)).then_inc(s_load, 16)
                sp.wait_ge(s_load, LOADS * u + LOADS)
                alone(sp)

            def load_maxima(b, f):
                u = 2 * b + f
                sp.wait_ge(maxT_ready, u + 1)
                alone(sp)
                sp.dma_start(max_dram[f].rearrange("i c a t -> (i c a) t"), maxT[f * P // 2:(f + 1) * P // 2]).then_inc(s_max_out, 16)
                sp.wait_ge(s_max_out, 16 * u + 16)
                alone(sp)
                sp.dma_start(f32(qs[f][4 * HD:ROWS]).rearrange("c a (i t) -> c a i t", i=QT),
                             max_dram[f].rearrange("i c a t -> c a i t")).then_inc(s_max_in, 16)
                sp.wait_ge(s_max_in, 16 * u + 16)
                alone(sp)

            def load_experts(pair, slot):
                sp.dma_start(w13f[:, slot], w13[bass.ds(pair, 1)].rearrange("o (c p) n -> p (o c) n", p=P)
                             ).then_inc(w_load[slot], 16)
                for h, row, f0, f1 in ((0, 0, 0, FF), (1, 0, 0, HIGH), (1, P // 2, HIGH, FF)):
                    sp.dma_start(w2f[row:row + f1 - f0, slot, h],
                                 w2[bass.ds(2 * pair + h, 1), f0:f1].rearrange("o f n -> f (o n)")
                                 ).then_inc(w_load[slot], 16)

            spill(0)
            load_stacks(0, 0)
            load_maxima(0, 0)
            load_stacks(0, 1)
            load_maxima(0, 1)
            load_experts(0, 0)
            load_experts(1, 1)
            with sp.Fori(0, BATCHES - 1) as b:
                spill(b + 1)
                for f in range(2):
                    load_stacks(b + 1, f)
                    load_maxima(b + 1, f)

            with sp.Fori(0, EFOURS - 1) as ep:
                for slot in range(2):
                    sp.wait_ge(w_split, 2 * ep + slot + 1)
                    load_experts(2 * ep + 2 + slot, slot)

            for t in range(0, TILES, 2):
                sp.wait_ge(fin_ready, t + 2)
                sp.dma_start(out[t // QT, (t % QT) * P:(t % QT + 2) * P, :].rearrange("(t p) e -> p t e", p=P),
                             ybuf[:, t:t + 2, :]).then_inc(s_out, 16)
            sp.wait_ge(s_out, 8 * TILES)


        @block.gpsimd
        def _(pool):
            for k, (buffer, value) in enumerate((
                    (maxhl[:], 0.0), (oT[:], 0.0), (w2f[:], 0.0), (f32(ks[0][4 * HD:ROWS]), 1.0), (f32(ks[1][4 * HD:ROWS]), 1.0),
                    (vs[:], 0.0), (vs[:, 0, :, :, 0::2, HD], 1.0), (vs[:, 1, :, :, 0::2, HD], 1.0))):
                if k:
                    pool.wait_ge(s_ones, k)
                nc.gpsimd.memset(buffer, value).then_inc(s_ones, 1)
            pool.wait_ge(s_prep, 1)

            def project(b, i, step):
                t = b * QT + i
                if step == 5:
                    pool.wait_ge(rope_parts, t + 1)
                    nc.gpsimd.tensor_tensor(rope_cos[:], rope_cos[:], rope_sin[:], ALU.add).then_inc(rope_done, 1)

            def close(b, i, step):
                T, r = b * QT + i, i % 2
                if step == 5:
                    pool.wait_ge(post_eps, T + 1)
                    nc.gpsimd.tensor_tensor(post_rstd[:, r:r + 1], post_var[:, r:r + 1], half[:, 0:1], ALU.pow
                                            ).then_inc(post_scale, 1)
                    pool.wait_ge(y_norm, T + 1)
                    tile = xt[:, bass.ds(T, 1), :].rearrange("p o e -> p (o e)")
                    nc.gpsimd.tensor_tensor(tile, tile, y_sb[:, r], ALU.add).then_inc(x1_ready, 1)
                if step == 7:
                    pool.wait_ge(post2_eps, T + 1)
                    nc.gpsimd.tensor_tensor(post_rstd[:, r:r + 1], post_var[:, r:r + 1], half[:, 0:1], ALU.pow
                                            ).then_inc(post2_scale, 1)

            def project_batch_norm(b):
                pool.wait_ge(ln1_eps, b + 1)
                nc.gpsimd.tensor_tensor(ln1_rstd[:], ln1_var[:], half[:], ALU.pow).then_inc(ln1_scale, 1)

            def weights_low(ep, slot):
                e = 2 * ep + slot
                pool.wait_ge(wh_made, 2 * e + 2)
                nc.gpsimd.tensor_tensor(w13l[:, slot], w13f[:, slot], f32(w13h[:, slot]), ALU.subtract)
                nc.gpsimd.tensor_tensor(w2l[:, slot], w2f[:, slot], f32(w2h[:, slot]), ALU.subtract
                                        ).then_inc(w_split, 1)

            def slot(b, f, side_project, side_close, before):
                for pos in range(NC):
                    if pos == 0 and side_project is not None:
                        project_batch_norm(side_project)
                    if side_project is not None:
                        for i, s in project_steps(pos):
                            project(side_project, i, s)
                    if side_close is not None:
                        for i, s in close_steps(pos):
                            close(side_close, i, s)

            project_batch_norm(0)
            for i in range(QT):
                project(0, i, 5)
            slot(0, 0, None, None, None)
            with pool.Fori(0, BATCHES - 1) as b:
                slot(b, 1, b + 1, None, (b, 0, NPAIR - 1))
                slot(b + 1, 0, None, b, (b, 1, NPAIR - 1))
            weights_low(0, 0)
            weights_low(0, 1)
            slot(BATCHES - 1, 1, None, None, (BATCHES - 1, 0, NPAIR - 1))
            for pos in range(NC):
                for i, s in close_steps(pos):
                    close(BATCHES - 1, i, s)

            pool.wait_ge(gates_ready, TILES)

            def hidden_low(ep, n):
                u = UNITS * ep + n
                pool.wait_ge(hidh_ready, u + 1)
                nc.gpsimd.tensor_tensor(hidl[:, n % 4], hid[:, n % 4], f32(hidh[:, n % 4]), ALU.subtract
                                        ).then_inc(hidl_ready, 1)

            pool.sem_inc(hidl_ready, 2)
            hidden_low(0, 0)
            hidden_low(0, 1)
            with pool.Fori(0, EFOURS - 1) as ep:
                for n in range(2, UNITS + 2):
                    hidden_low(ep + n // UNITS, n % UNITS)
                    if n == 5:
                        weights_low(ep + 1, 0)
                weights_low(ep + 1, 1)
            for n in range(2, UNITS):
                hidden_low(EFOURS - 1, n)

            for b in range(BATCHES):
                ts = slice(b * QT, b * QT + QT)
                pool.wait_ge(fin_eps, b + 1)
                nc.gpsimd.tensor_tensor(fin_rstd[:, ts], fin_var[:, ts], half[:], ALU.pow).then_inc(fin_scale, 1)
                for t in range(b * QT, b * QT + QT):
                    pool.wait_ge(fin_norm, t + 1)
                    nc.gpsimd.tensor_tensor(ybuf[:, t, :], ybuf[:, t, :], xt[:, t, :], ALU.add
                                            ).then_inc(fin_ready, 1)

        @block.scalar
        def _(act):
            act.sem_inc(exp_done, 2)

            def project(b, i, step):
                t = b * QT + i
                if step == 2:
                    act.wait_ge(xnT_psum, t + 1)
                    wait(act, qkv_psum, t)
                    nc.scalar.copy(xnT[:], bank[XT][:, 0:EMB].rearrange("p (c n) -> p c n", c=KC)
                                   ).then_inc(xnT_ready, 1)
                if step == 4:
                    act.wait_ge(qkv_psum, t + 1)
                    if i == 0:
                        wait(act, v_ready, 4 * b)
                    nc.scalar.copy(v_stage[:, i], bank[VB][:, 0:EMB].rearrange("p (h d) -> p h d", h=HEADS)
                                   ).then_inc(v_staged, 1)
                if step == 7:
                    act.wait_ge(qkT_psum, t + 1)
                    wait(act, s_spill, 32 * t)
                    nc.scalar.copy(qkTh[:], bank[SCORE[i % 2]][:, :].rearrange("p (w n) -> p w n", w=4)
                                   ).then_inc(qkTh_ready, 1)

            def place_v(b, f):
                act.wait_ge(v_staged, QT * b + QT)
                if not isinstance(b, int):
                    act.wait_ge(pv_psum, 2 * (2 * b + f - 1) * NPAIR + 4)
                for h in range(2):
                    nc.scalar.copy(vs[:, f, :, :, 2 * h, 0:HD], v_stage[:, :, f * HALF + h:(f + 1) * HALF:2]
                                   ).then_inc(v_ready, 1)

            def maxima_out(b, f):
                u = 2 * b + f
                act.wait_ge(maxT_psum, u + 1)
                wait(act, s_max_out, 16 * u)
                rows = slice(f * P // 2, (f + 1) * P // 2)
                nc.scalar.copy(maxT[rows], bank[SCORE[0]][rows, 0:P]).then_inc(maxT_ready, 1)

            def close(b, i, step):
                T, r = b * QT + i, i % 2
                if step == 2:
                    act.wait_ge(attnT_psum, T + 2)
                    nc.scalar.copy(attnT[:, r], bank[QK][:, 0:EMB].rearrange("p (c n) -> p c n", c=KC)
                                   ).then_inc(attnT_ready, 1)
                if step == 9:
                    act.wait_ge(xn2T_psum, T + 1)
                    xn2T = bank[XT][:, 0:EMB].rearrange("p (c n) -> p c n", c=KC)
                    nc.scalar.copy(x2T_tile[:, r], xn2T)
                    nc.scalar.copy(x2T[:, :, bass.ds(T * P, P)], xn2T).then_inc(x2T_ready, 1)
                if step == 11:
                    act.wait_ge(router_psum, T + 1)
                    nc.scalar.copy(logits[:, r], bank[XT][:, EMB:EMB + EXPERTS]).then_inc(logits_ready, 1)
                if step == 13:
                    act.wait_ge(negtop_ready, T + 1)
                    nc.scalar.activation(expl[:, r], logits[:, r], ACTF.Exp, bias=negtop[:, r:r + 1]
                                         ).then_inc(expl_ready, 1)

            def exponentials(b, f, c):
                u = 2 * b + f
                n = u * NC + c
                act.wait_ge(weigh_psum, n + 1)
                if c % 5 == 0:
                    act.wait_ge(pv_psum, 2 * (u * NPAIR + c // 5) + 2)
                nc.scalar.activation(probs[:, c % RING], bank[WEIGH[c % 2]][:, :], ACTF.Exp).then_inc(exp_done, 1)

            def copy_transposed(b, f, p):
                n = (2 * b + f) * NPAIR + p
                act.wait_ge(pv_psum, 2 * n + 6)
                nc.scalar.copy(oT[0:2 * VW], bank[OB][0:2 * VW, :]).then_inc(oT_ready, 1)

            def weights_high(ep, slot):
                act.wait_ge(w_load[slot], 64 * ep + 64)
                alone(act)
                nc.scalar.copy(w13h[:, slot], w13f[:, slot]).then_inc(wh_made, 1)
                nc.scalar.copy(w2h[:, slot], w2f[:, slot]).then_inc(wh_made, 1)

            def slot(b, f, side_project, side_close, before):
                for pos in range(NC):
                    if side_project is None and f == 0 and pos == 4:
                        place_v(b, 1)
                    exponentials(b, f, pos)
                    if pos == 1 and before is not None:
                        copy_transposed(*before)
                    if pos > 5 and pos % 5 == 1:
                        copy_transposed(b, f, pos // 5 - 1)
                    if side_project is not None:
                        for i, s in project_steps(pos):
                            project(side_project, i, s)
                        if pos == NC - 1:
                            place_v(side_project, 0)
                    if side_close is not None:
                        for i, s in close_steps(pos):
                            close(side_close, i, s)
                    if side_project is None and f == 0 and pos == 16:
                        maxima_out(b, 1)
                    if side_project is not None and pos == 18:
                        maxima_out(side_project, 0)

            for pos in range(NC):
                for i, s in project_steps(pos):
                    project(0, i, s)
            place_v(0, 0)
            maxima_out(0, 0)
            slot(0, 0, None, None, None)
            with act.Fori(0, BATCHES - 1) as b:
                slot(b, 1, b + 1, None, (b, 0, NPAIR - 1))
                slot(b + 1, 0, None, b, (b, 1, NPAIR - 1))
            weights_high(0, 0)
            weights_high(0, 1)
            slot(BATCHES - 1, 1, None, None, (BATCHES - 1, 0, NPAIR - 1))
            copy_transposed(BATCHES - 1, 1, NPAIR - 1)
            for pos in range(NC):
                for i, s in close_steps(pos):
                    close(BATCHES - 1, i, s)

            act.wait_ge(gates_ready, TILES)
            for c in range(CHUNKS):
                ts = slice(c * 512, c * 512 + 512)
                nc.scalar.copy(xh[:, :, ts], x2T[:, :, ts]).then_inc(xh_cut, 1)

            def unit(ep, n):
                u = UNITS * ep + n
                act.wait_ge(gu_psum, u + 1)
                nc.scalar.activation(silu[:, n % 2, 0], bank[n % 2][:, :], ACTF.Silu)
                nc.scalar.activation(silu[P // 2:P, n % 2, 1], bank[4 + n % 2][0:P // 2, :], ACTF.Silu
                                     ).then_inc(silu_ready, 1)
                act.wait_ge(hid_ready, u + 1)
                nc.scalar.copy(hidh[:, n % 4], hid[:, n % 4]).then_inc(hidh_ready, 1)

            unit(0, 0)
            unit(0, 1)
            with act.Fori(0, EFOURS - 1) as ep:
                for n in range(2, UNITS + 2):
                    unit(ep + n // UNITS, n % UNITS)
                    if n == 5:
                        act.wait_ge(down_psum, 4 * (UNITS * ep + CHUNKS))
                        weights_high(ep + 1, 0)
                act.wait_ge(down_psum, 4 * (UNITS * ep + UNITS))
                weights_high(ep + 1, 1)
            for n in range(2, UNITS):
                unit(EFOURS - 1, n)

        @block.vector
        def _(dve):
            dve.sem_inc(max_done, 2)
            nc.vector.memset(half[:], -0.5).then_inc(s_prep, 1)
            dve.wait_ge(s_const, 16 * 6)
            nc.vector.tensor_copy(ident_b[:], ident_f[:]).then_inc(s_prep, 1)
            nc.vector.tensor_copy(mask_b[:], mask_f).then_inc(s_prep, 1)

            def tile_of(buf, T):
                return buf[:, bass.ds(T, 1), :].rearrange("p o e -> p (o e)")

            def mean_var(n, stat, mv, var, src, s_bn, s_mean, s_eps):
                alone(dve)
                nc.vector.bn_stats(stat, src).then_inc(s_bn, 1)
                dve.wait_ge(s_bn, n + 1)
                alone(dve)
                nc.vector.bn_aggr(mv, stat).then_inc(s_mean, 1)
                dve.wait_ge(s_mean, n + 1)
                nc.vector.tensor_scalar(var, mv[:, 1:2], EPS, None, ALU.add).then_inc(s_eps, 1)

            def batch_norm_stats(b):
                dve.wait_ge(s_x, 16 * b + 16)
                alone(dve)
                for i in range(QT):
                    nc.vector.bn_stats(ln1_stat[:, i], tile_of(xt, b * QT + i)).then_inc(ln1_bn, 1)
                dve.wait_ge(ln1_bn, QT * b + QT)
                alone(dve)
                for i in range(QT):
                    nc.vector.bn_aggr(ln1_mv[:, i], ln1_stat[:, i]).then_inc(ln1_mean, 1)
                dve.wait_ge(ln1_mean, QT * b + QT)
                nc.vector.tensor_scalar(ln1_var[:], ln1_mv[:, :, 1], EPS, None, ALU.add).then_inc(ln1_eps, 1)

            def project(b, i, step):
                t = b * QT + i
                if step == 0:
                    if i == 0:
                        dve.wait_ge(ln1_scale, b + 1)
                    wait(dve, xnT_psum, t)
                    nc.vector.tensor_scalar(xn[:], tile_of(xt, t), ln1_mv[:, i, 0:1], ln1_rstd[:, i:i + 1],
                                            ALU.subtract, ALU.mult).then_inc(xn_ready, 1)
                if step == 4:
                    dve.wait_ge(qkv_psum, t + 1)
                    wait(dve, qkT_psum, t)
                    qk = bank[QK][:, :].rearrange("p (w h d) -> p w h d", w=2, h=HEADS)
                    cos = rope_sb[:, i, 0].unsqueeze(2)
                    sin = rope_sb[:, i, 1].unsqueeze(2)
                    nc.vector.tensor_tensor(rope_cos[:], qk, cos.broadcast_to([P, 2, HEADS, HD]), ALU.mult)
                    for o in range(2):
                        last = nc.vector.tensor_tensor(rope_sin[:, :, :, o::2], qk[:, :, :, 1 - o::2],
                                                       sin[:, :, :, o::2].broadcast_to([P, 2, HEADS, HD // 2]), ALU.mult)
                    last.then_inc(rope_parts, 1)
                if step == 7:
                    dve.wait_ge(qkTh_ready, t + 1)
                    wait(dve, s_spill, 32 * t)
                    nc.vector.tensor_tensor(qkTl[:], bank[SCORE[i % 2]][:, :].rearrange("p (w n) -> p w n", w=4),
                                            f32(qkTh[:]), ALU.subtract).then_inc(qkTl_ready, 1)

            def row_maxima(b, f, c):
                u = 2 * b + f
                dve.wait_ge(score_psum, u * NC + c + 1)
                if c == 0:
                    wait(dve, maxl_ready, u)
                places = PAIR_BANKS[c % 5]
                h0 = 2 * (c // 5)
                S = bank[SCORE[c % 2]]
                if len(places) == 2 and places[0][1] == places[1][1]:
                    i = places[0][1]
                    last = nc.vector.tensor_reduce(negmax[:, i, h0:h0 + 2], S[:, :].rearrange("p (a l) -> p a l", a=2),
                                                   AXX, ALU.max, negate=True)
                else:
                    for h, i, col in places:
                        last = nc.vector.tensor_reduce(negmax[:, i, h0 + h:h0 + h + 1], S[:, col:col + P * (i + 1)],
                                                       AXX, ALU.max, negate=True)
                last.then_inc(max_done, 1)

            def cut_maxima(b, f):
                u = 2 * b + f
                dve.wait_ge(max_done, u * NC + NC + 2)
                wait(dve, maxT_psum, u)
                nc.vector.tensor_copy(maxhl[:, f, :, 0, :].bitcast(F32R), negmax[:]).then_inc(maxh_ready, 1)
                dve.wait_ge(maxh_ready, u + 1)
                nc.vector.tensor_tensor(maxhl[:, f, :, 1, :], negmax[:], maxhl[:, f, :, 0, :], ALU.subtract
                                        ).then_inc(maxl_ready, 1)

            def normalise(b, f, p):
                n = (2 * b + f) * NPAIR + p
                dve.wait_ge(o_psum, n + 1)
                O = bank[OB][:, :].rearrange("p (i n) -> p i n", i=QT)[:, :, 0:2 * VW].rearrange("p i (a v) -> p a i v", a=2)
                wait(dve, attn_ready, n)
                nc.vector.reciprocal(o_inv[:], O[:, :, :, HD]).then_inc(inv_ready, 1)
                goal = attn[:, :, HALF + 2 * p:HALF + 2 * p + 2] if f == 1 else attn_first[:, :, 2 * p:2 * p + 2]
                dve.wait_ge(inv_ready, n + 1)
                nc.vector.tensor_tensor(goal.rearrange("p i a d -> p a i d"), O[:, :, :, 0:HD],
                                        o_inv[:].unsqueeze(3).broadcast_to([P, 2, QT, HD]), ALU.mult
                                        ).then_inc(attn_ready, 1)

            def join_halves(b):
                dve.wait_ge(attn_ready, (2 * b + 1) * NPAIR)
                dve.wait_ge(attnT_psum, QT * b + 1)
                nc.vector.tensor_copy(attn[:, :, 0:HALF], attn_first[:]).then_inc(joined, 1)

            def close(b, i, step):
                T, r = b * QT + i, i % 2
                if step == 4:
                    dve.wait_ge(wo_psum, T + 1)
                    mean_var(T, post_stat[:, r], post_mv[:, r], post_var[:, r:r + 1], bank[VB][:, 0:EMB],
                             post_bn, post_mean, post_eps)
                if step == 5:
                    dve.wait_ge(post_scale, T + 1)
                    nc.vector.tensor_scalar(y_sb[:, r], bank[VB][:, 0:EMB], post_mv[:, r, 0:1], post_rstd[:, r:r + 1],
                                            ALU.subtract, ALU.mult).then_inc(y_norm, 1)
                if step == 6:
                    dve.wait_ge(x1_ready, T + 1)
                    mean_var(T, post_stat[:, r], post_mv[:, r], post_var[:, r:r + 1], tile_of(xt, T),
                             post2_bn, post2_mean, post2_eps)
                if step == 7:
                    dve.wait_ge(post2_scale, T + 1)
                    nc.vector.tensor_scalar(xn2[:, r], tile_of(xt, T), post_mv[:, r, 0:1], post_rstd[:, r:r + 1],
                                            ALU.subtract, ALU.mult).then_inc(xn2_ready, 1)
                if step == 12:
                    dve.wait_ge(logits_ready, T + 1)
                    alone(dve)
                    nc.vector.max(top[:, r], logits[:, r]).then_inc(top_ready, 1)
                    dve.wait_ge(top_ready, T + 1)
                    nc.vector.tensor_scalar(negtop[:, r:r + 1], top[:, r, 0:1], -1.0, None, ALU.mult
                                            ).then_inc(negtop_ready, 1)
                    nc.vector.match_replace(struck[:, r], top[:, r], logits[:, r], -3.0e38).then_inc(struck_ready, 1)
                    dve.wait_ge(struck_ready, T + 1)
                    nc.vector.tensor_tensor(chosen[:, r], struck[:, r], logits[:, r], ALU.not_equal
                                            ).then_inc(chosen_ready, 1)
                if step == 13:
                    dve.wait_ge(expl_ready, T + 1)
                    dve.wait_ge(chosen_ready, T + 1)
                    nc.vector.tensor_tensor(picked[:, r], expl[:, r], chosen[:, r], ALU.mult).then_inc(picked_ready, 1)
                    dve.wait_ge(picked_ready, T + 1)
                    nc.vector.reduce_sum(gsum[:, r:r + 1], picked[:, r], AXX).then_inc(gsum_ready, 1)
                    dve.wait_ge(gsum_ready, T + 1)
                    nc.vector.reciprocal(ginv[:, r:r + 1], gsum[:, r:r + 1]).then_inc(ginv_ready, 1)
                    dve.wait_ge(ginv_ready, T + 1)
                    nc.vector.tensor_scalar(tile_of(gates, T), picked[:, r], ginv[:, r:r + 1], None, ALU.mult
                                            ).then_inc(gates_ready, 1)

            def slot(b, f, side_project, side_close, before):
                for pos in range(NC):
                    if pos == 0 and side_project is not None:
                        batch_norm_stats(side_project)
                    if pos == 3 and before is not None:
                        normalise(*before)
                        if f == 1:
                            join_halves(b)
                    if pos > 5 and pos % 5 == 3:
                        normalise(b, f, pos // 5 - 1)
                    if side_project is not None:
                        for i, s in project_steps(pos):
                            project(side_project, i, s)
                        for c in late_scores(pos):
                            row_maxima(side_project, 0, c)
                        if pos == 17:
                            cut_maxima(side_project, 0)
                    elif f == 0:
                        for c in early_scores(pos):
                            row_maxima(b, 1, c)
                        if pos == 15:
                            cut_maxima(b, 1)
                    if side_close is not None:
                        for i, s in close_steps(pos):
                            close(side_close, i, s)

            batch_norm_stats(0)
            for pos in range(NC):
                for i, s in project_steps(pos):
                    project(0, i, s)
            for c in range(NC):
                row_maxima(0, 0, c)
            cut_maxima(0, 0)
            slot(0, 0, None, None, None)
            with dve.Fori(0, BATCHES - 1) as b:
                slot(b, 1, b + 1, None, (b, 0, NPAIR - 1))
                slot(b + 1, 0, None, b, (b, 1, NPAIR - 1))
            slot(BATCHES - 1, 1, None, None, (BATCHES - 1, 0, NPAIR - 1))
            normalise(BATCHES - 1, 1, NPAIR - 1)
            for pos in range(NC):
                for i, s in close_steps(pos):
                    close(BATCHES - 1, i, s)

            dve.wait_ge(gates_ready, TILES)
            for c in range(CHUNKS):
                ts = slice(c * 512, c * 512 + 512)
                dve.wait_ge(xh_cut, c + 1)
                nc.vector.tensor_tensor(xl[:, :, ts], x2T[:, :, ts], f32(xh[:, :, ts]), ALU.subtract
                                        ).then_inc(xl_cut, 1)
            nc.vector.memset(hid[:], 0.0)
            for c in range(2):
                nc.vector.memset(acc[:, c * TILES // 2:(c + 1) * TILES // 2], 0.0).then_inc(acc_done, 1)

            def hidden(ep, n, first=False):
                u = UNITS * ep + n
                dve.wait_ge(silu_ready, u + 1)
                if not first:
                    dve.wait_ge(hidl_ready, u - 1)
                for h, to, part, up, r0, r1 in ((0, 0, 0, 2, 0, FF), (1, 0, 0, 2, FF, P), (1, P // 2, 1, 4, P // 2, P)):
                    last = nc.vector.tensor_tensor(hid[to:to + r1 - r0, n % 4, h], silu[r0:r1, n % 2, part],
                                                   bank[up + n % 2][r0:r1, :], ALU.mult)
                last.then_inc(hid_ready, 1)

            def gather_up(ep, n, h):
                u = UNITS * ep + n
                e = 2 * (2 * ep + n // CHUNKS) + h
                c = n % CHUNKS
                for k in range(4):
                    if k % 2 == 0:
                        dve.wait_ge(down_psum, 4 * u + 2 * h + k // 2 + 1)
                        dve.wait_ge(acc_done, 4 * u + 2 * h + k // 2 + 2)
                    t = 4 * c + k
                    r = nc.vector.scalar_tensor_tensor(
                        acc[:, t, :], bank[6 + k // 2][:, (k % 2) * EMB:(k % 2 + 1) * EMB],
                        gates[:, t, bass.ds(e, 1)], acc[:, t, :], ALU.mult, ALU.add)
                    if k % 2:
                        r.then_inc(acc_done, 1)

            def final_stats(b):
                ts = range(b * QT, b * QT + QT)
                dve.wait_ge(acc_done, 4 * (UNITS * (EFOURS - 1) + CHUNKS + b + 1) + 2)
                alone(dve)
                for t in ts:
                    nc.vector.bn_stats(fin_stat[:, t], acc[:, t, :]).then_inc(fin_bn, 1)
                dve.wait_ge(fin_bn, QT * b + QT)
                alone(dve)
                for t in ts:
                    nc.vector.bn_aggr(fin_mv[:, t], fin_stat[:, t]).then_inc(fin_mean, 1)
                dve.wait_ge(fin_mean, QT * b + QT)
                nc.vector.tensor_scalar(fin_var[:, ts[0]:ts[0] + QT], fin_mv[:, ts[0]:ts[0] + QT, 1], EPS, None, ALU.add
                                        ).then_inc(fin_eps, 1)

            def final_norm(b):
                dve.wait_ge(fin_scale, b + 1)
                for t in range(b * QT, b * QT + QT):
                    nc.vector.tensor_scalar(ybuf[:, t, :], acc[:, t, :], fin_mv[:, t, 0:1], fin_rstd[:, t:t + 1],
                                            ALU.subtract, ALU.mult).then_inc(fin_norm, 1)

            dve.wait_ge(acc_done, 2)
            hidden(0, 0, first=True)
            hidden(0, 1, first=True)
            with dve.Fori(0, EFOURS - 1) as ep:
                for n in range(2, UNITS + 2):
                    gather_up(ep, n - 2, 0)
                    gather_up(ep, n - 2, 1)
                    hidden(ep + n // UNITS, n % UNITS)
            ep = EFOURS - 1
            for n in range(2, UNITS + 2):
                gather_up(ep, n - 2, 0)
                gather_up(ep, n - 2, 1)
                if n < UNITS:
                    hidden(ep, n)
                if n - 2 >= CHUNKS:
                    final_stats(n - 2 - CHUNKS)
                if n - 3 >= CHUNKS:
                    final_norm(n - 3 - CHUNKS)
            final_norm(BATCHES - 1)

        @block.tensor
        def _(pe):
            pe.sem_inc(pv_psum, 4)
            pe.sem_inc(attnT_psum, 1)
            pe.wait_ge(s_const, 16 * 6)
            pe.wait_ge(s_prep, 3)
            pe.wait_ge(s_ones, 8)

            def transpose2(dst, src):
                for c in range(KC):
                    last = nc.tensor.matmul(dst[:, c * P:(c + 1) * P], src[:, c * P:(c + 1) * P], ident_f[:],
                                            is_transpose=True, start=True, stop=True)
                return last

            def product(dst, a, w):
                for c in range(KC):
                    last = nc.tensor.matmul(dst, a[:, c], w[:, c], start=(c == 0), stop=(c == KC - 1))
                return last

            def project(b, i, step):
                t = b * QT + i
                if step == 1:
                    pe.wait_ge(xn_ready, t + 1)
                    wait(pe, xnT_ready, t)
                    transpose2(bank[XT], xn).then_inc(xnT_psum, 1)
                if step == 3:
                    pe.wait_ge(xnT_ready, t + 1)
                    wait(pe, rope_parts, t)
                    wait(pe, v_staged, t)
                    product(bank[QK][:, :], xnT, wqkv_sb[:, :, 0:2 * EMB])
                    product(bank[VB][:, 0:EMB], xnT, wqkv_sb[:, :, 2 * EMB:]).then_inc(qkv_psum, 1)
                if step == 6:
                    pe.wait_ge(rope_done, t + 1)
                    wait(pe, qkTl_ready, t)
                    for w in range(4):
                        last = nc.tensor.matmul(
                            bank[SCORE[i % 2]][:, w * P:(w + 1) * P],
                            rope_cos[:, w // 2, (w % 2) * HALF:(w % 2 + 1) * HALF].rearrange("p h d -> p (h d)"),
                            ident_f[:], is_transpose=True, start=True, stop=True)
                    last.then_inc(qkT_psum, 1)

            def add_masks(S, cols, a, w):
                first, last = cols[0] // P, cols[-1] // P
                blocks = S[:, :].rearrange("p (a n) -> p a n", n=P)[:, first:last + 1:max(last - first, 1)]
                nc.tensor.matmul(blocks, a[:], w[:].unsqueeze(1).broadcast_to([P, len(cols), P]),
                                 start=True, stop=False, skip_group_check=True)

            def scores(b, f, c):
                u = 2 * b + f
                if c == 0:
                    pe.wait_ge(s_load, LOADS * u + LOADS)
                    wait(pe, maxT_ready, u)
                pe.wait_ge(max_done, u * NC + c + 1)
                S = bank[SCORE[c % 2]]
                add_masks(S, [col + P * i for h, i, col in PAIR_BANKS[c % 5]], ident_b, mask_b)
                for h, i, col in PAIR_BANKS[c % 5]:
                    a = 2 * (c // 5) + h
                    L = P * (i + 1)
                    last = nc.tensor.matmul(S[:, col:col + L], qs[f][:, a, i * P:(i + 1) * P], ks[f][:, a, 0:L],
                                            start=False, stop=True, skip_group_check=True)
                last.then_inc(score_psum, 1)

            def transpose_maxima(b, f):
                u = 2 * b + f
                pe.wait_ge(maxl_ready, u + 1)
                wait(pe, maxT_ready, u)
                nc.tensor.matmul(bank[SCORE[0]][:, 0:P],
                                 maxhl[:].rearrange("p f i c a -> p (f i c a)"), ident_f[:],
                                 is_transpose=True, start=True, stop=True).then_inc(maxT_psum, 1)

            def weigh(b, f, c):
                u = 2 * b + f
                if c == 0:
                    pe.wait_ge(s_max_in, 16 * u + 16)
                pe.wait_ge(exp_done, u * NC + c + 1)
                S = bank[WEIGH[c % 2]]
                add_masks(S, [col for h, r, col in PAIR_BANKS[c % 5]], mask_b, ident_b)
                for h, r, col in PAIR_BANKS[c % 5]:
                    a = 2 * (c // 5) + h
                    j, N = QT - 1 - r, P * (r + 1)
                    last = nc.tensor.matmul(S[:, col:col + N], ks[f][:, a, j * P:(j + 1) * P], qs[f][:, a, j * P:],
                                            start=False, stop=True, skip_group_check=True)
                last.then_inc(weigh_psum, 1)

            def weigh_values(b, f, p, h):
                u = 2 * b + f
                n = u * NPAIR + p
                if h == 0:
                    if p == 0:
                        pe.wait_ge(v_ready, 2 * u + 2)
                    wait(pe, attn_ready, n)
                pe.wait_ge(exp_done, u * NC + 5 * p + 3 + 2 * h + 2)
                for j in range(QT):
                    w, col = KPLACE[(h, j)]
                    last = nc.tensor.matmul(
                        bank[OB][0:2 * VW, j * P:], vs[:, f, j, p, h:h + 2].rearrange("p a v -> p (a v)"),
                        probs[:, (5 * p + w) % RING, col:col + (QT - j) * P], start=(h == 0 and j == 0),
                        stop=(h == 1 and j == QT - 1), skip_group_check=True)
                last.then_inc(pv_psum, 1)

            def transpose_output(b, f, p):
                n = (2 * b + f) * NPAIR + p
                pe.wait_ge(oT_ready, n + 1)
                for i in range(QT):
                    last = nc.tensor.matmul(bank[OB][:, i * P:(i + 1) * P], oT[:, i * P:(i + 1) * P], ident_f[:],
                                            is_transpose=True, start=True, stop=True)
                last.then_inc(o_psum, 1)

            def close(b, i, step):
                T, r = b * QT + i, i % 2
                if step == 1:
                    pe.wait_ge(attn_ready, 2 * NPAIR * (b + 1))
                    pe.wait_ge(joined, b + 1)
                    if i > 0:
                        pe.wait_ge(attnT_ready, T)
                    transpose2(bank[QK], attn[:, i].rearrange("p h d -> p (h d)")).then_inc(attnT_psum, 1)
                if step == 3:
                    pe.wait_ge(attnT_ready, T + 1)
                    if i > 0:
                        pe.wait_ge(y_norm, T)
                    product(bank[VB][:, 0:EMB], attnT[:, r], wo_sb).then_inc(wo_psum, 1)
                if step == 8:
                    pe.wait_ge(xn2_ready, T + 1)
                    if i > 0:
                        pe.wait_ge(logits_ready, T)
                    transpose2(bank[XT][:, 0:EMB], xn2[:, r]).then_inc(xn2T_psum, 1)
                if step == 10:
                    pe.wait_ge(x2T_ready, T + 1)
                    product(bank[XT][:, EMB:EMB + EXPERTS], x2T_tile[:, r], wg_sb).then_inc(router_psum, 1)

            def slot(b, f, side_project, side_close, before):
                weigh(b, f, 0)
                for pos in range(NC):
                    if pos + 1 < NC:
                        weigh(b, f, pos + 1)
                    if pos == 0 and before is not None:
                        weigh_values(*before, 1)
                    if pos == 2 and before is not None:
                        transpose_output(*before)
                    if pos % 5 == 4:
                        weigh_values(b, f, pos // 5, 0)
                    if pos >= 5 and pos % 5 == 0:
                        weigh_values(b, f, pos // 5 - 1, 1)
                    if pos >= 5 and pos % 5 == 2:
                        transpose_output(b, f, pos // 5 - 1)
                    if side_project is not None:
                        for i, s in project_steps(pos):
                            project(side_project, i, s)
                        for c in late_scores(pos):
                            scores(side_project, 0, c)
                        if pos == 18:
                            transpose_maxima(side_project, 0)
                    elif f == 0:
                        for c in early_scores(pos):
                            scores(b, 1, c)
                        if pos == 16:
                            transpose_maxima(b, 1)
                    if side_close is not None:
                        for i, s in close_steps(pos):
                            close(side_close, i, s)

            for pos in range(NC):
                for i, s in project_steps(pos):
                    project(0, i, s)
            for c in range(NC):
                scores(0, 0, c)
            transpose_maxima(0, 0)
            slot(0, 0, None, None, None)
            with pe.Fori(0, BATCHES - 1) as b:
                slot(b, 1, b + 1, None, (b, 0, NPAIR - 1))
                slot(b + 1, 0, None, b, (b, 1, NPAIR - 1))
            slot(BATCHES - 1, 1, None, None, (BATCHES - 1, 0, NPAIR - 1))
            weigh_values(BATCHES - 1, 1, NPAIR - 1, 1)
            transpose_output(BATCHES - 1, 1, NPAIR - 1)
            for pos in range(NC):
                for i, s in close_steps(pos):
                    close(BATCHES - 1, i, s)

            FIRST = ((0, 0), (0, 1), (1, 0))
            SECOND = ((1, 1), (2, 0), (2, 1))

            def gate_up(ep, n, parts, first=False):
                u = UNITS * ep + n
                slot, c = n // CHUNKS, n % CHUNKS
                if (0, 0) in parts:
                    if c == 0:
                        pe.wait_ge(w_split, 2 * ep + slot + 1)
                    if not first:
                        pe.wait_ge(hid_ready, u - 1)
                for part, kc in parts:
                    for k, (w, xx) in enumerate(((w13h, xh), (w13h, xl), (w13l, xh))):
                        r = nc.tensor.matmul(bank[2 * part + n % 2][:, :], w[:, slot, kc, part * P:(part + 1) * P],
                                             xx[:, kc, c * 512:(c + 1) * 512], start=(kc == 0 and k == 0),
                                             stop=(kc == KC - 1 and k == 2))
                if (2, 1) in parts:
                    r.then_inc(gu_psum, 1)

            def down(ep, n, h):
                u = UNITS * ep + n
                slot = n // CHUNKS
                pe.wait_ge(hidh_ready, u + 1)
                pe.wait_ge(hidl_ready, u + 3)
                for k in range(4):
                    if k % 2 == 0:
                        pe.wait_ge(acc_done, 4 * u + 2 * h + k // 2 + 1)
                    dst = bank[6 + k // 2][:, (k % 2) * EMB:(k % 2 + 1) * EMB]
                    for m, (hh, w) in enumerate(((hidh, w2h), (hidh, w2l), (hidl, w2h))):
                        r = nc.tensor.matmul(dst, hh[:, n % 4, h, k * P:(k + 1) * P], w[:, slot, h, :],
                                             start=(m == 0), stop=(m == 2))
                    if k % 2:
                        r.then_inc(down_psum, 1)

            pe.wait_ge(gates_ready, TILES)
            pe.wait_ge(xl_cut, 1)
            gate_up(0, 0, FIRST + SECOND, first=True)
            pe.wait_ge(xl_cut, 2)
            gate_up(0, 1, FIRST + SECOND, first=True)
            pe.wait_ge(xl_cut, CHUNKS)
            with pe.Fori(0, EFOURS - 1) as ep:
                for n in range(2, UNITS + 2):
                    gate_up(ep + n // UNITS, n % UNITS, FIRST)
                    down(ep, n - 2, 0)
                    gate_up(ep + n // UNITS, n % UNITS, SECOND)
                    down(ep, n - 2, 1)
            ep = EFOURS - 1
            for n in range(2, UNITS + 2):
                if n < UNITS:
                    gate_up(ep, n, FIRST)
                down(ep, n - 2, 0)
                if n < UNITS:
                    gate_up(ep, n, SECOND)
                down(ep, n - 2, 1)



_INS = ['L0_attn_x', 'L0_attn_Wqkv', 'L0_attn_Wo', 'L0_ffn_wg', 'L0_ffn_w1', 'L0_ffn_v1', 'L0_ffn_w2']


def kernel(**inputs):
    import numpy as np
    import concourse.bacc as bacc
    from concourse import mybir as mb
    from concourse.bass_utils import run_bass_kernel_spmd

    x, wqkv, wo, wg, w1, v1, w2 = (np.ascontiguousarray(inputs[n]) for n in _INS)
    f = np.float32
    inv = (f(1.0) / np.power(f(10000.0), f(2.0) * np.arange(HD // 2, dtype=f) / f(HD))).astype(f)
    angle = np.outer(np.arange(SEQ, dtype=f), inv).astype(f)
    cos, sin = np.cos(angle).astype(f), np.sin(angle).astype(f)
    table = np.stack([np.repeat(cos, 2, axis=1), np.stack([-sin, sin], axis=2).reshape(SEQ, HD)], axis=1)
    rope = np.ascontiguousarray(np.stack([table * f(0.25), table], axis=2))
    arrays = {
        "x": x, "wqkv": wqkv, "wo": wo,
        "wgT": np.ascontiguousarray(wg.T),
        "w13": np.ascontiguousarray(np.concatenate(
            [w1[0::2], w1[1::2, :, :HIGH], v1[0::2], v1[1::2, :, :HIGH], w1[1::2, :, HIGH:], v1[1::2, :, HIGH:]], axis=2)),
        "w2": w2,
        "ident": np.eye(P, dtype=f),
        "mask": np.triu(np.full((P, P), -1e30, dtype=f), 1),
        "rope": rope,
    }
    nc = bacc.Bacc("TRN2", target_bir_lowering=False, num_devices=1)
    args = [nc.dram_tensor(n, a.shape, mb.dt.from_np(a.dtype), kind="ExternalInput").ap() for n, a in arrays.items()]
    args.append(nc.dram_tensor("out", (BATCHES, SEQ, EMB), mb.dt.float32, kind="ExternalOutput").ap())
    build(nc, *args)
    r = run_bass_kernel_spmd(nc, [arrays], core_ids=[0])
    return r.results[0]["out"]
```
